# Optimizing a Trainium2 kernel written in Bass

```python
import numpy as np
import jax
import jax.numpy as jnp

def _softmax(x, axis=-1):
    return jax.nn.softmax(x, axis=axis)

def _gelu(x):
    return jax.nn.gelu(x, approximate=True)

def _silu(x):
    return jax.nn.silu(x)

def _sigmoid(x):
    return jax.nn.sigmoid(x)

def _layernorm(x, axis=-1, eps=1e-05):
    m = jnp.mean(x, axis=axis, keepdims=True)
    v = jnp.var(x, axis=axis, keepdims=True)
    return (x - m) / jnp.sqrt(v + eps)

def _scatter_add(tgt, idx, src, axis=0):
    return tgt.at[idx].add(src)

def _segment_sum(src, seg, n):
    return jax.ops.segment_sum(src, seg, n)
kernel_name = 'mk_audio_tower_d1_tok_audfeat256_r4_e6fe4e'

def setup_inputs(seed: int=0):
    np.random.seed(seed)
    _w = jnp.asarray

    def _rec_inputs():
        import jax
        import jax.numpy as jnp
        _rk = jax.random.key(seed)
        x = jax.random.uniform(jax.random.fold_in(_rk, 1), (8, 4, 256), jnp.float32, 0.0, 0.999986)
        return x
    x = _rec_inputs()

    def _L0_tok_setup():
        import jax, jax.numpy as jnp
        import numpy as np
        T = 8
        key = jax.random.key(seed)
        ks = jax.random.split(key, 9)
        bs, dims, L, d = (16, 4, 512, 64)
        x = jax.random.uniform(ks[0], (bs, dims, L), dtype=jnp.float32)
        s_in = 1.0 / np.sqrt(dims)
        s_d = 1.0 / np.sqrt(d)
        W1 = jax.random.uniform(ks[1], (d, dims), minval=-s_in, maxval=s_in, dtype=jnp.float32)
        b1 = jax.random.uniform(ks[2], (d,), minval=-s_in, maxval=s_in, dtype=jnp.float32)
        W2 = jax.random.uniform(ks[3], (d, d), minval=-s_d, maxval=s_d, dtype=jnp.float32)
        b2 = jax.random.uniform(ks[4], (d,), minval=-s_d, maxval=s_d, dtype=jnp.float32)
        W3 = jax.random.uniform(ks[5], (d, dims), minval=-s_in, maxval=s_in, dtype=jnp.float32)
        b3 = jax.random.uniform(ks[6], (d,), minval=-s_in, maxval=s_in, dtype=jnp.float32)
        W4 = jax.random.uniform(ks[7], (d, d), minval=-s_d, maxval=s_d, dtype=jnp.float32)
        b4 = jax.random.uniform(ks[8], (d,), minval=-s_d, maxval=s_d, dtype=jnp.float32)
        return dict(x=x, W1=W1, b1=b1, W2=W2, b2=b2, W3=W3, b3=b3, W4=W4, b4=b4)
    _L0_tok_all = _L0_tok_setup()
    _L0_tok_in = {k: v for k, v in _L0_tok_all.items() if k in ('W1', 'b1', 'W2', 'b2', 'W3', 'b3', 'W4', 'b4')}
    del _L0_tok_all

    def _L0_attn_setup():
        import jax, jax.numpy as jnp
        import numpy as np
        D_ATT = 64
        D_GROUP = 32
        N_GROUP = D_ATT // D_GROUP
        key = jax.random.key(seed)
        ks = jax.random.split(key, 6)
        B, L = (4, 128)
        import math
        s = 1.0 / math.sqrt(D_ATT)
        return {'x': jax.random.normal(ks[0], (B, L, D_ATT), dtype=jnp.float32), 'Wq': jax.random.normal(ks[1], (D_ATT, D_ATT), dtype=jnp.float32) * s * 0.06, 'Wk': jax.random.normal(ks[2], (D_ATT, D_ATT), dtype=jnp.float32) * s * 0.06, 'Wv': jax.random.normal(ks[3], (D_ATT, D_ATT), dtype=jnp.float32) * s * 0.06, 'w_mlp': jax.random.normal(ks[4], (D_GROUP,), dtype=jnp.float32) * 0.1, 'b_mlp': jax.random.normal(ks[5], (1,), dtype=jnp.float32) * 0.1}
    _L0_attn_all = _L0_attn_setup()
    _L0_attn_in = {k: v for k, v in _L0_attn_all.items() if k in ('Wq', 'Wk', 'Wv', 'w_mlp', 'b_mlp')}
    del _L0_attn_all

    def _L0_ffn_setup():
        import jax, jax.numpy as jnp
        import numpy as np
        TOP_K = 2
        key = jax.random.key(seed)
        ks = jax.random.split(key, 4)
        B, L, D, H, E = (8, 1024, 64, 256, 8)
        s = 0.02
        return {'x': jax.random.normal(ks[0], (B, L, D), jnp.float32), 'Wg': jax.random.normal(ks[1], (D, E), jnp.float32) * s, 'bg': jnp.zeros((E,), jnp.float32), 'W1': jax.random.normal(ks[2], (E, D, H), jnp.float32) * s, 'b1': jnp.zeros((E, H), jnp.float32), 'W2': jax.random.normal(ks[3], (E, H, D), jnp.float32) * s, 'b2': jnp.zeros((E, D), jnp.float32)}
    _L0_ffn_all = _L0_ffn_setup()
    _L0_ffn_in = {k: v for k, v in _L0_ffn_all.items() if k in ('Wg', 'bg', 'W1', 'b1', 'W2', 'b2')}
    del _L0_ffn_all
    return {'x': x, 'L0_tok_W1': _L0_tok_in['W1'], 'L0_tok_b1': _L0_tok_in['b1'], 'L0_tok_W2': _L0_tok_in['W2'], 'L0_tok_b2': _L0_tok_in['b2'], 'L0_tok_W3': _L0_tok_in['W3'], 'L0_tok_b3': _L0_tok_in['b3'], 'L0_tok_W4': _L0_tok_in['W4'], 'L0_tok_b4': _L0_tok_in['b4'], 'L0_attn_Wq': _L0_attn_in['Wq'], 'L0_attn_Wk': _L0_attn_in['Wk'], 'L0_attn_Wv': _L0_attn_in['Wv'], 'L0_attn_w_mlp': _L0_attn_in['w_mlp'], 'L0_attn_b_mlp': _L0_attn_in['b_mlp'], 'L0_ffn_Wg': _L0_ffn_in['Wg'], 'L0_ffn_bg': _L0_ffn_in['bg'], 'L0_ffn_W1': _L0_ffn_in['W1'], 'L0_ffn_b1': _L0_ffn_in['b1'], 'L0_ffn_W2': _L0_ffn_in['W2'], 'L0_ffn_b2': _L0_ffn_in['b2']}

def reference(x, L0_tok_W1, L0_tok_b1, L0_tok_W2, L0_tok_b2, L0_tok_W3, L0_tok_b3, L0_tok_W4, L0_tok_b4, L0_attn_Wq, L0_attn_Wk, L0_attn_Wv, L0_attn_w_mlp, L0_attn_b_mlp, L0_ffn_Wg, L0_ffn_bg, L0_ffn_W1, L0_ffn_b1, L0_ffn_W2, L0_ffn_b2):
    import jax
    import jax.numpy as jnp

    def _L0_tok_ref(x, W1, b1, W2, b2, W3, b3, W4, b4):
        import jax, jax.numpy as jnp
        import numpy as np
        T = 8
        a = jnp.einsum('bdl,od->blo', x, W1) + b1
        bs, L, d = a.shape
        zcol = jnp.zeros((bs, 1, d), a.dtype)
        shift_r = lambda v: jnp.concatenate([zcol, v[:, :-1]], axis=1)
        shift_l = lambda v: jnp.concatenate([v[:, 1:], zcol], axis=1)
        up = jnp.zeros_like(a)
        down = jnp.zeros_like(a)
        for _ in range(T):
            up = jax.nn.relu(a + shift_r(up) @ W2.T + b2)
            down = jax.nn.relu(a + shift_l(down) @ W2.T + b2)
        c = jnp.einsum('bdl,od->blo', x, W3) + b3
        miu = jax.nn.relu(c + (shift_r(up) @ W4.T + b4) + (shift_l(down) @ W4.T + b4))
        return miu

    def _L0_attn_ref(x, Wq, Wk, Wv, w_mlp, b_mlp):
        import jax, jax.numpy as jnp
        import numpy as np
        D_ATT = 64
        D_GROUP = 32
        N_GROUP = D_ATT // D_GROUP
        B, L, d_att = x.shape
        G, Dg = (N_GROUP, D_GROUP)
        Q = x @ Wq.T
        K = x @ Wk.T
        V = x @ Wv.T
        Qg = Q.reshape(B, L, 1, G, Dg)
        Kg = K.reshape(B, 1, L, G, Dg)
        diff = Qg - Kg
        attn = jnp.einsum('bqkgd,d->bqkg', jax.nn.relu(diff), w_mlp) + b_mlp[0]
        attn = jax.nn.relu(attn)
        attn = jax.nn.softmax(attn, axis=2)
        Vg = V.reshape(B, L, Dg, G)
        out = jnp.einsum('bqkg,bkdg->bqdg', attn, Vg)
        return out.reshape(B, L, d_att)

    def _L0_ffn_ref(x, Wg, bg, W1, b1, W2, b2):
        import jax, jax.numpy as jnp
        import numpy as np
        TOP_K = 2
        B, L, D = x.shape
        E = W1.shape[0]
        xf = x.reshape(-1, D)
        gate_logits = xf @ Wg + bg
        top_w, top_i = jax.lax.top_k(gate_logits, TOP_K)
        top_w = jax.nn.softmax(top_w, axis=-1)
        w_dense = jnp.sum(jax.nn.one_hot(top_i, E, dtype=xf.dtype) * top_w[..., None], axis=1)
        out = jnp.zeros_like(xf)
        for e in range(E):
            h = jax.nn.gelu(xf @ W1[e] + b1[e], approximate=False)
            out = out + w_dense[:, e:e + 1] * (h @ W2[e] + b2[e])
        return out.reshape(B, L, D)
    h = _L0_tok_ref(x, L0_tok_W1, L0_tok_b1, L0_tok_W2, L0_tok_b2, L0_tok_W3, L0_tok_b3, L0_tok_W4, L0_tok_b4)
    h = h + _L0_attn_ref(_layernorm(h, axis=-1), L0_attn_Wq, L0_attn_Wk, L0_attn_Wv, L0_attn_w_mlp, L0_attn_b_mlp)
    h = h + _L0_ffn_ref(_layernorm(h, axis=-1), L0_ffn_Wg, L0_ffn_bg, L0_ffn_W1, L0_ffn_b1, L0_ffn_W2, L0_ffn_b2)
    return h

_drawn_inputs = setup_inputs


def setup_inputs(seed=0):
    import zlib

    import numpy as np

    out = dict(_drawn_inputs(seed))
    spreads = {'L0_ffn_bg': (0.0, 0.1), 'L0_ffn_b1': (0.0, 0.317), 'L0_ffn_b2': (0.0, 0.1)}
    factors = {'L0_attn_Wq': 110.905, 'L0_attn_Wk': 24.644, 'L0_attn_w_mlp': 8.0}
    for name, (base, spread) in spreads.items():
        noise = np.random.default_rng([zlib.crc32(name.encode()), seed]).standard_normal(out[name].shape)
        drawn = base * np.exp(spread * noise) if base else spread * noise
        out[name] = jnp.asarray(drawn.astype(out[name].dtype))
    for name, factor in factors.items():
        out[name] = (out[name] * factor).astype(out[name].dtype)
    return out
```

```python
from contextlib import ExitStack

import concourse.bass as bass
from concourse import mybir

ALU = mybir.AluOpType
ACT = mybir.ActivationFunctionType
F32 = mybir.dt.float32
BF16 = mybir.dt.bfloat16
U32 = mybir.dt.uint32
AX = mybir.AxisListType

B, DIN, L = 8, 4, 256
D, E, H = 64, 8, 256
G, DG = 2, 32
T = 8
EPS = 1e-5
P = 128
PAIRS = B // 2
TOK = 2 * L
TT = TOK // P
BLOCKS = 4
SLOTS = 32
RING = 6
K9 = 9
KX = 75
HT = H // P
EULER = 2.718281828459045


def act_share(g):
    return (3,) if g % 3 == 1 else (2, 3)


def build(nc, x9, w9, sel9, tokw, ident_d, fold_d, iota_d, wa_d, wf_d, wd_d, b1_d, b2_d, bg_d, bm_d,
          wsc_d, gates_dram, out_d):
    with ExitStack() as ctx:
        def sb(name, shape, dt=F32):
            return ctx.enter_context(nc.sbuf_tensor(name, shape, dt))

        def sem(name):
            return ctx.enter_context(nc.semaphore(name))

        x_sb = sb("x_sb", [K9, PAIRS * TOK])
        x_res = sb("x_res", [K9, PAIRS * TOK])
        x_pc = sb("x_pc", [K9, 3, PAIRS * TOK], BF16)
        w_sb = sb("w_sb", [K9, 2, 192])
        w_res = sb("w_res", [K9, 192])
        w_pc = sb("w_pc", [K9, 3, 192], BF16)
        sel_f = sb("sel_f", [K9, 6 * KX])
        sel = sb("sel", [K9, 6, KX], BF16)
        ws = sb("ws", [KX, 192], BF16)
        tokw_sb = sb("tokw_sb", [P, 192])
        ident = sb("ident", [P, P])
        ident_b = sb("ident_b", [P, P], BF16)
        fold = sb("fold", [P, D])
        iota8 = sb("iota8", [P, E])
        wa_sb = sb("wa_sb", [P, 192])
        wa_res = sb("wa_res", [P, 192])
        wa_hi = sb("wa_hi", [P, 192], BF16)
        wa_mid = sb("wa_mid", [P, 192], BF16)
        wa_lh = sb("wa_lh", [P, 192], BF16)
        NF = E * H + E
        wf_sb = sb("wf_sb", [P, NF])
        wf_hi = sb("wf_hi", [P, NF], BF16)
        wf_mid = sb("wf_mid", [P, NF], BF16)
        wf_lh = sb("wf_lh", [P, NF], BF16)
        wd = sb("wd", [P, E, HT, D])
        b1 = sb("b1", [P, E * HT])
        b2 = sb("b2", [P, E // 2])
        bg = sb("bg", [P, E])
        bm = sb("bm", [P, 1])
        neg_bm = sb("neg_bm", [P, 1])
        wsc = sb("wsc", [P, 8, 32])
        ones32 = sb("ones32", [P, 32])
        neg_half = sb("neg_half", [P, TT])
        euler = sb("euler", [P, TT])

        xs = sb("xs", [KX, TOK], BF16)
        state = sb("state", [P, 2, L + 1])
        last = sb("last", [P, 2, L + 1])
        h1 = sb("h1", [P, 2, TT, D])
        stats = sb("stats", [P, 2, TT, 6])
        mv = sb("mv", [P, 2, TT, 2])
        rstd = sb("rstd", [P, 2, TT])
        xn = sb("xn", [P, 2, TT, D])
        xn_res = sb("xn_res", [P, 2, TT, D])
        xn_pc = sb("xn_pc", [P, 2, TT, 4, D], BF16)
        xa = sb("xa", [P, 2, TOK], BF16)
        q_sb = sb("q_sb", [P, 2, L])
        nk_sb = sb("nk_sb", [P, 2, L])
        v_sb = sb("v_sb", [P, 2, TT, G, DG])

        relu_ring = sb("relu_ring", [P, RING, 4, 2, L])
        sc_sb = sb("sc_sb", [P, 2, 2 * BLOCKS, L])
        mx = sb("mx", [P, 2, 2 * BLOCKS])
        nmx = sb("nmx", [P, 2 * BLOCKS])
        pt = sb("pt", [P, 2, 4, BLOCKS, 2, 32])
        rec = sb("rec", [P, L])
        att = sb("att", [P, L])
        h2 = sb("h2", [P, TT, D])

        xf = sb("xf", [P, 2, TOK], BF16)
        lg = sb("lg", [P, TT, E])
        top = sb("top", [P, TT, 8])
        topi = sb("topi", [P, TT, 8], U32)
        topf = sb("topf", [P, TT, 2])
        gap = sb("gap", [P, TT])
        egap = sb("egap", [P, TT])
        gden = sb("gden", [P, TT])
        gw = sb("gw", [P, TT, 2])
        oh = sb("oh", [P, 2, TT, E])
        wdense = sb("wdense", [P, TT, E])
        wt_sb = sb("wt_sb", [E, TOK])
        wbc = sb("wbc", [P, E // 2, TOK])
        hid = sb("hid", [P, 8, TOK])
        prod = sb("prod", [P, 2, TOK])
        acc = sb("acc", [P, TOK])
        o_sb = sb("o_sb", [P, TT, D])

        bank = [ctx.enter_context(nc.psum_tensor(f"bank{i}", [P, 512], F32)) for i in range(8)]
        SCORE, TOKB, UPB, DOWNB, MISC = (0, 1), (2, 3), (4, 5), 6, 7

        ld_tok = sem("ld_tok"); ld_cst = sem("ld_cst"); ld_wa = sem("ld_wa"); ld_att = sem("ld_att")
        ld_ffn = sem("ld_ffn")
        consts_set = sem("consts_set")
        sel_ready = sem("sel_ready"); wpc_ready = sem("wpc_ready"); ws_mm = sem("ws_mm")
        ws_ready = sem("ws_ready")
        xpc0_ready = sem("xpc0_ready"); xpc_ready = sem("xpc_ready")
        wa_ready = sem("wa_ready"); wf_ready = sem("wf_ready"); identb_ready = sem("identb_ready")
        nbm_ready = sem("nbm_ready")
        xs_mm = sem("xs_mm"); xs_ready = sem("xs_ready")
        tok_mm = [sem("tok_mm0"), sem("tok_mm1")]
        tok_relu = [sem("tok_relu0"), sem("tok_relu1")]
        h1_mm = sem("h1_mm"); h1_ready = sem("h1_ready"); h1_stats = sem("h1_stats")
        xn1_ready = sem("xn1_ready"); xa_mm = sem("xa_mm"); xa_ready = sem("xa_ready")
        qk_mm = sem("qk_mm"); v_mm = sem("v_mm"); qk_ready = sem("qk_ready"); v_ready = sem("v_ready")
        relu_dve = sem("relu_dve"); relu_act = sem("relu_act"); score_mm = sem("score_mm")
        score_kept = sem("score_kept"); nmx_ready = sem("nmx_ready"); exp_ready = sem("exp_ready")
        pt_mm = sem("pt_mm"); pt_ready = sem("pt_ready"); pv_mm = sem("pv_mm")
        att_ready = sem("att_ready"); att_t = sem("att_t"); h2_ready = sem("h2_ready")
        h2_stats = sem("h2_stats"); xn2_ready = sem("xn2_ready"); xf_mm = sem("xf_mm")
        xf_ready = sem("xf_ready"); gate_mm = sem("gate_mm"); lg_ready = sem("lg_ready")
        gap_ready = sem("gap_ready"); egap_ready = sem("egap_ready"); w_ready = sem("w_ready")
        wt_mm = sem("wt_mm"); wt_ready = sem("wt_ready"); wbc_ready = sem("wbc_ready")
        up_mm = sem("up_mm"); gelu_ready = sem("gelu_ready"); down_mm = sem("down_mm")
        prod_ready = sem("prod_ready"); acc_ready = sem("acc_ready"); fold_mm = sem("fold_mm")
        gates_out = sem("gates_out"); out_ready = sem("out_ready"); out_stored = sem("out_stored")
        dve_step = sem("dve_step"); pool_step = sem("pool_step")

        block = ctx.enter_context(nc.Block())

        def chain(eng, step):
            count = [0]

            def link(ins):
                count[0] += 1
                ins.then_inc(step, 1)
                eng.wait_ge(step, count[0])
            return link

        def norm_split(eng, vec, link, src, k):
            link(vec.tensor_scalar(rstd[:, k], mv[:, k, :, 1], EPS, None, ALU.add))
            link(nc.gpsimd.tensor_tensor(rstd[:, k], rstd[:, k], neg_half[:], ALU.pow))
            link(vec.tensor_tensor(xn[:, k], src, mv[:, k, :, 0:1].broadcast_to([P, TT, D]),
                                   ALU.subtract))
            link(vec.tensor_tensor(xn[:, k], xn[:, k],
                                   rstd[:, k, :, None].broadcast_to([P, TT, D]), ALU.mult))
            link(vec.tensor_copy(xn_pc[:, k, :, 0], xn[:, k]))
            vec.tensor_copy(xn_pc[:, k, :, 2], xn_pc[:, k, :, 0])
            link(vec.tensor_tensor(xn_res[:, k], xn[:, k], xn_pc[:, k, :, 0], ALU.subtract))
            link(vec.tensor_copy(xn_pc[:, k, :, 1], xn_res[:, k]))
            return vec.tensor_tensor(xn_pc[:, k, :, 3], xn_res[:, k], xn_pc[:, k, :, 1], ALU.subtract)

        @block.sync
        def _(sp):
            for dst, src in ((w_sb[:], w9), (sel_f[:], sel9), (x_sb[:], x9), (tokw_sb[:], tokw)):
                sp.dma_start(dst, src).then_inc(ld_tok, 16)
            for dst, src in ((wa_sb[:], wa_d), (ident[:], ident_d)):
                sp.dma_start(dst, src).then_inc(ld_wa, 16)
            for dst, src in ((wsc[:], wsc_d), (bm[:], bm_d.partition_broadcast(P))):
                sp.dma_start(dst, src).then_inc(ld_att, 16)
            for dst, src in ((wf_sb[:], wf_d), (wd[:], wd_d), (b1[:], b1_d), (b2[:], b2_d),
                             (bg[:], bg_d.partition_broadcast(P)), (fold[:], fold_d),
                             (iota8[:], iota_d)):
                sp.dma_start(dst, src).then_inc(ld_ffn, 16)
            for p in range(PAIRS):
                sp.wait_ge(wt_ready, p + 1)
                if p >= 1:
                    sp.wait_ge(prod_ready, 4 * p)
                sp.dma_start(gates_dram[p], wt_sb[:]).then_inc(gates_out, 16)
                sp.wait_ge(gates_out, 16 * (p + 1))
                for half in range(2):
                    sp.dma_start(wbc[64 * half:64 * half + 64],
                                 gates_dram[p].rearrange("(a h) t -> h a t", h=2)[half].partition_broadcast(64)
                                 ).then_inc(wbc_ready, 16)
                sp.wait_ge(out_ready, p + 1)
                sp.dma_start(out_d[p], o_sb[:]).then_inc(out_stored, 16)
            sp.wait_ge(out_stored, 16 * PAIRS)

        @block.gpsimd
        def _(pool):
            link = chain(pool, pool_step)
            vec = nc.gpsimd
            vec.memset(neg_half[:], -0.5)
            vec.memset(euler[:], EULER)
            vec.memset(ones32[:], 1.0)
            vec.memset(state[:, :, 0:1], 0.0)
            vec.memset(last[:], 0.0).then_inc(consts_set, 1)
            pool.wait_ge(consts_set, 1)

            def norm1(p):
                pool.wait_ge(h1_stats, p + 1)
                if p >= 1:
                    pool.wait_ge(xa_mm, p)
                norm_split(pool, vec, link, h1[:, p % 2], 0).then_inc(xn1_ready, 1)

            def norm2(p):
                pool.wait_ge(h2_stats, p + 1)
                if p >= 1:
                    pool.wait_ge(xf_mm, p)
                norm_split(pool, vec, link, h2[:], 1).then_inc(xn2_ready, 1)

            def gate_exp(p):
                pool.wait_ge(gap_ready, p + 1)
                vec.tensor_tensor(egap[:], euler[:], gap[:], ALU.pow).then_inc(egap_ready, 1)

            def expert_sum(p):
                for ep in range(E // 2):
                    pool.wait_ge(prod_ready, 4 * p + ep + 1)
                    if ep == 0:
                        if p >= 1:
                            pool.wait_ge(fold_mm, p)
                        vec.tensor_copy(acc[:], prod[:, 0]).then_inc(acc_ready, 1)
                    else:
                        pool.wait_ge(acc_ready, 4 * p + ep)
                        vec.tensor_tensor(acc[:], acc[:], prod[:, ep % 2],
                                          ALU.add).then_inc(acc_ready, 1)

            norm1(0)
            c = slice(TOK, PAIRS * TOK)
            link(vec.tensor_copy(x_pc[:, 0, c], x_sb[:, c]))
            link(vec.tensor_tensor(x_res[:, c], x_sb[:, c], x_pc[:, 0, c], ALU.subtract))
            link(vec.tensor_copy(x_pc[:, 1, c], x_res[:, c]))
            vec.tensor_tensor(x_pc[:, 2, c], x_res[:, c], x_pc[:, 1, c],
                              ALU.subtract).then_inc(xpc_ready, 1)
            pool.wait_ge(ld_ffn, 16 * 7)
            link(vec.tensor_copy(wf_hi[:], wf_sb[:]))
            link(vec.tensor_copy(wf_lh[64:128], wf_hi[64:128]))
            link(vec.tensor_tensor(wf_sb[:], wf_sb[:], wf_hi[:], ALU.subtract))
            link(vec.tensor_copy(wf_mid[:], wf_sb[:]))
            vec.tensor_tensor(wf_lh[0:64], wf_sb[0:64], wf_mid[0:64],
                              ALU.subtract).then_inc(wf_ready, 1)
            for p in range(PAIRS):
                if p >= 1:
                    norm2(p - 1)
                    gate_exp(p - 1)
                if p + 1 < PAIRS:
                    norm1(p + 1)
                if p >= 1:
                    expert_sum(p - 1)
            norm2(PAIRS - 1)
            gate_exp(PAIRS - 1)
            expert_sum(PAIRS - 1)

        @block.scalar
        def _(act):
            def stack_inputs(p):
                act.wait_ge(xs_mm, p + 1)
                nc.scalar.copy(xs[:], bank[TOKB[0]][0:KX, :]).then_inc(xs_ready, 1)

            def tok_step(p, t):
                act.wait_ge(tok_mm[0], T * p + t + 1)
                src = bank[TOKB[0]]
                if t < T - 1:
                    nc.scalar.activation(state[:, 0, 1:L + 1], src[:, 0:L],
                                         ACT.Relu).then_inc(tok_relu[0], 1)
                else:
                    nc.scalar.activation(last[0:64, 0, 1:L], src[0:64, 0:L - 1],
                                         ACT.Relu).then_inc(tok_relu[0], 1)
                    nc.scalar.activation(last[64:128, 0, L - 2::-1], src[64:128, 0:L - 1],
                                         ACT.Relu).then_inc(tok_relu[0], 1)

            def token_out(p):
                act.wait_ge(h1_mm, p + 1)
                if p >= 2:
                    act.wait_ge(h2_ready, p - 1)
                nc.scalar.activation(h1[:, p % 2], bank[TOKB[0]][:, 0:TT * D], ACT.Relu
                                     ).then_inc(h1_ready, 1)

            def keep_qk(p):
                act.wait_ge(qk_mm, p + 1)
                if p >= 2:
                    act.wait_ge(relu_dve, SLOTS * (p - 1))
                src = bank[TOKB[0]]
                nc.scalar.copy(q_sb[:, p % 2, :], src[:, 0:L]).then_inc(qk_ready, 1)
                nc.scalar.mul(nk_sb[:, p % 2, :], src[:, L:2 * L], -1.0).then_inc(qk_ready, 1)

            def relu_tiles(p, g):
                n = SLOTS * p + g
                if n >= RING:
                    act.wait_ge(score_mm, n - RING + 1)
                for j in act_share(g):
                    for qi in range(2):
                        q = (g // 8) * 64 + qi * 32 + j * 8 + g % 8
                        ins = nc.scalar.activation(relu_ring[:, n % RING, j, qi, :], nk_sb[:, p % 2, :],
                                                   ACT.Relu, bias=q_sb[:, p % 2, q:q + 1])
                ins.then_inc(relu_act, 1)

            def exps(p):
                act.wait_ge(nmx_ready, p + 1)
                for blk in range(BLOCKS):
                    for qi in range(2):
                        c = 2 * blk + qi
                        ins = nc.scalar.activation(sc_sb[:, p % 2, c, :], sc_sb[:, p % 2, c, :], ACT.Exp,
                                                   bias=nmx[:, c:c + 1])
                    ins.then_inc(exp_ready, 1)

            def gelu(p, i):
                n = 16 * p + i
                act.wait_ge(up_mm, n + 1)
                if n >= 8:
                    act.wait_ge(down_mm, (n - 8) // 4 + 1)
                ep, r = i // 4, i % 4
                col = (2 * ep + r % 2) * HT + r // 2
                nc.scalar.activation(hid[:, n % 8, :], bank[UPB[n % 2]][:], ACT.Gelu,
                                     bias=b1[:, col:col + 1]).then_inc(gelu_ready, 1)

            def keep_wt(p):
                act.wait_ge(wt_mm, p + 1)
                if p >= 1:
                    act.wait_ge(gates_out, 16 * p)
                nc.scalar.copy(wt_sb[:], bank[MISC][0:E, :]).then_inc(wt_ready, 1)

            act.wait_ge(ws_mm, 1)
            nc.scalar.copy(ws[:], bank[TOKB[1]][0:KX, 0:192]).then_inc(ws_ready, 1)
            stack_inputs(0)
            for t in range(T):
                tok_step(0, t)
            token_out(0)
            keep_qk(0)
            act.wait_ge(qk_ready, 2)
            for p in range(PAIRS):
                if p >= 1:
                    act.wait_ge(qk_ready, 2 * (p + 1))
                for g in range(SLOTS):
                    if p >= 1:
                        if g == 4:
                            exps(p - 1)
                        if g == 22:
                            act.wait_ge(ld_ffn, 16 * 7)
                        if 22 <= g < 30:
                            gelu(p - 1, 2 * (g - 22))
                            gelu(p - 1, 2 * (g - 22) + 1)
                        if g == 24:
                            keep_wt(p - 1)
                    if p + 1 < PAIRS:
                        if g == 1:
                            stack_inputs(p + 1)
                        if g % 2 == 1 and 3 <= g < 3 + 2 * T:
                            tok_step(p + 1, (g - 3) // 2)
                        if g == 20:
                            token_out(p + 1)
                        if g == 29:
                            keep_qk(p + 1)
                    relu_tiles(p, g)
            exps(PAIRS - 1)
            for i in range(4):
                gelu(PAIRS - 1, i)
            keep_wt(PAIRS - 1)
            for i in range(4, 16):
                gelu(PAIRS - 1, i)

        @block.vector
        def _(dve):
            link = chain(dve, dve_step)
            vec = nc.vector

            def tok_step(p, t):
                dve.wait_ge(tok_mm[1], T * p + t + 1)
                src = bank[TOKB[1]]
                if t < T - 1:
                    vec.tensor_scalar(state[:, 1, 1:L + 1], src[:, 0:L], 0.0, None,
                                      ALU.max).then_inc(tok_relu[1], 1)
                else:
                    vec.tensor_scalar(last[0:64, 1, 1:L], src[0:64, 0:L - 1], 0.0, None,
                                      ALU.max).then_inc(tok_relu[1], 1)
                    vec.tensor_scalar(last[64:128, 1, L - 2::-1], src[64:128, 0:L - 1], 0.0, None,
                                      ALU.max).then_inc(tok_relu[1], 1)

            def token_stats(src, k):
                for i in range(TT):
                    ins = vec.bn_stats(stats[:, k, i, :], src[:, i, :])
                link(ins)
                for i in range(TT):
                    ins = vec.bn_aggr(mv[:, k, i, :], stats[:, k, i, :])
                return ins

            def stats1(p):
                dve.wait_ge(h1_ready, p + 1)
                if p >= 1:
                    dve.wait_ge(xn1_ready, p)
                token_stats(h1[:, p % 2], 0).then_inc(h1_stats, 1)

            def keep_xa(p):
                dve.wait_ge(xa_mm, p + 1)
                if p >= 1:
                    dve.wait_ge(v_mm, p)
                    dve.wait_ge(qk_mm, p)
                vec.tensor_copy(xa[:].rearrange("p a t -> p (a t)"), bank[TOKB[1]][:].bitcast(BF16)
                                ).then_inc(xa_ready, 1)

            def keep_v(p):
                dve.wait_ge(v_mm, p + 1)
                if p >= 2:
                    dve.wait_ge(pv_mm, p - 1)
                vec.tensor_copy(v_sb[:, p % 2].rearrange("p t g d -> p (t g d)"),
                                bank[TOKB[1]][:, 0:TT * D]).then_inc(v_ready, 1)

            def relu_tiles(p, g):
                n = SLOTS * p + g
                if n >= RING:
                    dve.wait_ge(score_mm, n - RING + 1)
                for j in range(4):
                    if j in act_share(g):
                        continue
                    for qi in range(2):
                        q = (g // 8) * 64 + qi * 32 + j * 8 + g % 8
                        ins = vec.tensor_scalar(relu_ring[:, n % RING, j, qi, :], nk_sb[:, p % 2, :],
                                                q_sb[:, p % 2, q:q + 1], 0.0, ALU.add, ALU.max)
                ins.then_inc(relu_dve, 1)

            def keep_scores(p, blk):
                dve.wait_ge(score_mm, SLOTS * p + 8 * (blk + 1))
                if p >= 2:
                    dve.wait_ge(pt_mm, 4 * (p - 2) + blk + 1)
                for qi in range(2):
                    c = 2 * blk + qi
                    ins = vec.tensor_scalar(sc_sb[:, p % 2, c, :],
                                            bank[SCORE[blk % 2]][:, qi * L:(qi + 1) * L],
                                            neg_bm[:, 0:1], None, ALU.max, ALU.max,
                                            accum_out=mx[:, p % 2, c:c + 1])
                ins.then_inc(score_kept, 1)

            def neg_max(p):
                dve.wait_ge(score_kept, 4 * (p + 1))
                if p >= 1:
                    dve.wait_ge(exp_ready, 4 * p)
                vec.tensor_scalar(nmx[:], mx[:, p % 2], -1.0, None, ALU.mult).then_inc(nmx_ready, 1)

            def keep_pt(p, blk):
                dve.wait_ge(pt_mm, 4 * p + blk + 1)
                if p >= 1 and blk == 0:
                    dve.wait_ge(pv_mm, p)
                for kh in range(2):
                    ins = vec.tensor_copy(
                        pt[:, kh, :, blk].rearrange("p b q j -> p q j b"),
                        bank[MISC][:, 256 * kh:256 * kh + 256].rearrange("p (q j b) -> p q j b", q=2, b=4))
                ins.then_inc(pt_ready, 1)

            def weigh(p):
                dve.wait_ge(pv_mm, p + 1)
                if p >= 1:
                    dve.wait_ge(att_t, p)
                link(vec.reciprocal(rec[:], bank[MISC][:, L:2 * L]))
                vec.tensor_tensor(att[:], bank[MISC][:, 0:L], rec[:], ALU.mult).then_inc(att_ready, 1)

            def residual1(p):
                dve.wait_ge(att_t, p + 1)
                if p >= 1:
                    dve.wait_ge(out_ready, p)
                for half in range(2):
                    src = bank[MISC][:, 128 * half:128 * half + 128].rearrange(
                        "p (b g d) -> p b g d", b=2, g=G)
                    old = h1[:, p % 2].rearrange("p (b h) (d g) -> p h b g d", h=2, g=G)[:, half]
                    new = h2[:].rearrange("p (b h) (d g) -> p h b g d", h=2, g=G)[:, half]
                    ins = vec.tensor_tensor(new, src, old, ALU.add)
                ins.then_inc(h2_ready, 1)
                dve.wait_ge(h2_ready, p + 1)
                token_stats(h2, 1).then_inc(h2_stats, 1)

            def keep_xf(p):
                dve.wait_ge(xf_mm, p + 1)
                if p >= 1:
                    dve.wait_ge(up_mm, 16 * p)
                vec.tensor_copy(xf[:].rearrange("p a t -> p (a t)"), bank[DOWNB][:].bitcast(BF16)
                                ).then_inc(xf_ready, 1)

            def top2(p):
                dve.wait_ge(gate_mm, p + 1)
                ins = vec.tensor_tensor(lg[:], bank[MISC][:, 0:TT * E].rearrange("p (t e) -> p t e", e=E),
                                        bg[:, None, :].broadcast_to([P, TT, E]), ALU.add)
                ins.then_inc(lg_ready, 1)
                dve.wait_ge(lg_ready, p + 1)
                for i in range(TT):
                    ins = vec.max(top[:, i, :], lg[:, i, :])
                link(ins)
                vec.tensor_tensor(gap[:], top[:, :, 1], top[:, :, 0], ALU.subtract
                                  ).then_inc(gap_ready, 1)
                for i in range(TT):
                    ins = vec.max_index(topi[:, i, :], top[:, i, :], lg[:, i, :])
                link(ins)
                link(vec.tensor_copy(topf[:], topi[:, :, 0:2]))
                for k in range(2):
                    ins = vec.tensor_tensor(oh[:, k], iota8[:, None, :].broadcast_to([P, TT, E]),
                                            topf[:, :, k:k + 1].broadcast_to([P, TT, E]), ALU.is_equal)
                link(ins)

            def gate_weights(p):
                dve.wait_ge(egap_ready, p + 1)
                link(vec.tensor_scalar(gden[:], egap[:], 1.0, None, ALU.add))
                link(vec.reciprocal(gw[:, :, 0], gden[:]))
                link(vec.tensor_tensor(gw[:, :, 1], gw[:, :, 0], egap[:], ALU.mult))
                for k in range(2):
                    ins = vec.tensor_tensor(oh[:, k], oh[:, k],
                                            gw[:, :, k:k + 1].broadcast_to([P, TT, E]), ALU.mult)
                link(ins)
                vec.tensor_tensor(wdense[:], oh[:, 0], oh[:, 1], ALU.add).then_inc(w_ready, 1)

            def weigh_expert(p, ep):
                n = 4 * p + ep
                dve.wait_ge(down_mm, n + 1)
                dve.wait_ge(wbc_ready, 32 * (p + 1))
                if n >= 2:
                    dve.wait_ge(acc_ready, n - 1)
                vec.scalar_tensor_tensor(prod[:, n % 2], bank[DOWNB][:], b2[:, ep:ep + 1], wbc[:, ep, :],
                                         ALU.add, ALU.mult).then_inc(prod_ready, 1)

            def residual2(p):
                dve.wait_ge(fold_mm, p + 1)
                if p >= 1:
                    dve.wait_ge(out_stored, 16 * p)
                vec.tensor_tensor(o_sb[:].rearrange("p t d -> p (t d)"), bank[MISC][:, 0:TT * D],
                                  h2[:].rearrange("p t d -> p (t d)"), ALU.add).then_inc(out_ready, 1)

            dve.wait_ge(ld_tok, 16 * 4)
            vec.tensor_copy(sel[:].rearrange("k s n -> k (s n)"), sel_f[:]).then_inc(sel_ready, 1)
            c = slice(0, TOK)
            link(vec.tensor_copy(x_pc[:, 0, c], x_sb[:, c]))
            link(vec.tensor_tensor(x_res[:, c], x_sb[:, c], x_pc[:, 0, c], ALU.subtract))
            link(vec.tensor_copy(x_pc[:, 1, c], x_res[:, c]))
            vec.tensor_tensor(x_pc[:, 2, c], x_res[:, c], x_pc[:, 1, c],
                              ALU.subtract).then_inc(xpc0_ready, 1)
            link(vec.tensor_tensor(w_sb[:, 0], w_sb[:, 0], w_sb[:, 1], ALU.add))
            link(vec.tensor_tensor(w_sb[:, 0, 128:], w_sb[:, 0, 128:], w_sb[:, 1, 128:], ALU.add))
            link(vec.tensor_copy(w_pc[:, 0], w_sb[:, 0]))
            link(vec.tensor_tensor(w_res[:], w_sb[:, 0], w_pc[:, 0], ALU.subtract))
            link(vec.tensor_copy(w_pc[:, 1], w_res[:]))
            vec.tensor_tensor(w_pc[:, 2], w_res[:], w_pc[:, 1], ALU.subtract).then_inc(wpc_ready, 1)
            dve.wait_ge(ld_wa, 32)
            vec.tensor_copy(ident_b[:], ident[:]).then_inc(identb_ready, 1)
            link(vec.tensor_copy(wa_hi[:], wa_sb[:]))
            vec.tensor_copy(wa_lh[64:128], wa_hi[64:128])
            link(vec.tensor_tensor(wa_res[:], wa_sb[:], wa_hi[:], ALU.subtract))
            link(vec.tensor_copy(wa_mid[:], wa_res[:]))
            vec.tensor_tensor(wa_lh[0:64], wa_res[0:64], wa_mid[0:64], ALU.subtract
                              ).then_inc(wa_ready, 1)
            dve.wait_ge(ld_att, 32)
            link(vec.tensor_scalar(neg_bm[:], bm[:], -1.0, None, ALU.mult))
            dve.wait_ge(consts_set, 1)
            for t in range(T):
                tok_step(0, t)
            stats1(0)
            keep_xa(0)
            keep_v(0)
            for p in range(PAIRS):
                dve.wait_ge(qk_ready, 2 * (p + 1))
                for g in range(SLOTS):
                    if g in (10, 18, 26):
                        keep_scores(p, g // 8 - 1)
                    if p >= 1:
                        if g == 2:
                            keep_scores(p - 1, 3)
                            neg_max(p - 1)
                        if 7 <= g < 11:
                            keep_pt(p - 1, g - 7)
                        if g == 12:
                            weigh(p - 1)
                        if g == 14:
                            residual1(p - 1)
                        if g == 19:
                            keep_xf(p - 1)
                        if g == 21:
                            dve.wait_ge(ld_ffn, 16 * 7)
                            top2(p - 1)
                        if g == 22:
                            gate_weights(p - 1)
                        if g in (25, 27, 29, 31):
                            weigh_expert(p - 1, (g - 25) // 2)
                    if p + 1 < PAIRS:
                        if g % 2 == 1 and 3 <= g < 3 + 2 * T:
                            tok_step(p + 1, (g - 3) // 2)
                        if g == 21:
                            stats1(p + 1)
                        if g == 27:
                            keep_xa(p + 1)
                        if g == 29:
                            keep_v(p + 1)
                    relu_tiles(p, g)
                if p >= 1:
                    residual2(p - 1)
            p = PAIRS - 1
            keep_scores(p, 3)
            neg_max(p)
            for blk in range(BLOCKS):
                keep_pt(p, blk)
            weigh(p)
            residual1(p)
            keep_xf(p)
            top2(p)
            gate_weights(p)
            for ep in range(E // 2):
                weigh_expert(p, ep)
            residual2(p)

        @block.tensor
        def _(pe):
            mm = nc.tensor.matmul

            def stack_inputs(p):
                if p == 0:
                    pe.wait_ge(xpc0_ready, 1)
                else:
                    pe.wait_ge(xpc_ready, 1)
                    pe.wait_ge(qk_ready, 2 * p)
                for i in range(3):
                    ins = mm(bank[TOKB[0]][0:KX, :], sel[:, i, :], x_pc[:, i, p * TOK:(p + 1) * TOK],
                             start=(i == 0), stop=(i == 2))
                ins.then_inc(xs_mm, 1)

            def tok_step(p, t):
                for b in range(2):
                    if t == 0:
                        if b == 0:
                            pe.wait_ge(xs_ready, p + 1)
                        elif p >= 1:
                            pe.wait_ge(v_ready, p)
                    else:
                        pe.wait_ge(tok_relu[b], (T + 1) * p + t)
                    dst = bank[TOKB[b]][:, 0:L]
                    if t > 0:
                        mm(dst, tokw_sb[:, 0:P], state[:, b, 0:L], start=True, stop=False)
                    mm(dst, ws[:, 0:P], xs[:, b * L:(b + 1) * L], start=(t == 0),
                       stop=True).then_inc(tok_mm[b], 1)

            def token_out(p):
                for b in range(2):
                    pe.wait_ge(tok_relu[b], (T + 1) * (p + 1))
                for b in range(2):
                    for h in range(2):
                        dst = bank[TOKB[0]][:, D * (2 * b + h):D * (2 * b + h + 1)]
                        mm(dst, last[:, b, P * h:P * (h + 1)], tokw_sb[:, P:P + D], start=True, stop=False)
                        ins = mm(dst, xs[:, b * L + P * h:b * L + P * (h + 1)], ws[:, P:P + D],
                                 start=False, stop=True)
                ins.then_inc(h1_mm, 1)

            def transpose_pieces(dst, k):
                view = dst[:].bitcast(BF16)
                for s in range(2):
                    for i in range(TT):
                        ins = nc.tensor.transpose(view[:, 512 * s + P * i:512 * s + P * (i + 1)],
                                                  xn_pc[:, k, i, 2 * s:2 * s + 2, :].rearrange("p a d -> p (a d)"),
                                                  ident_b[:])
                return ins

            def transpose_xn1(p):
                pe.wait_ge(xn1_ready, p + 1)
                transpose_pieces(bank[TOKB[1]], 0).then_inc(xa_mm, 1)

            def project(p):
                pe.wait_ge(xa_ready, p + 1)
                pe.wait_ge(h1_ready, p + 1)
                terms = ((wa_hi, 0), (wa_mid, 0), (wa_lh, 1))
                for c in range(2):
                    for n, (w, s) in enumerate(terms):
                        for b in range(2):
                            ins = mm(bank[TOKB[0]][64 * b:64 * b + 64, L * c:L * (c + 1)],
                                     w[:, D * c:D * (c + 1)], xa[:, s, L * b:L * (b + 1)],
                                     start=(n == 0), stop=(n == 2))
                ins.then_inc(qk_mm, 1)
                for i in range(TT):
                    for n, (w, s) in enumerate(terms):
                        ins = mm(bank[TOKB[1]][:, D * i:D * (i + 1)], xa[:, s, P * i:P * (i + 1)],
                                 w[:, 2 * D:3 * D], start=(n == 0), stop=(n == 2))
                ins.then_inc(v_mm, 1)

            def scores(n):
                p, g = n // SLOTS, n % SLOTS
                blk, s = g // 8, g % 8
                if s == 0 and 4 * p + blk >= 2:
                    pe.wait_ge(score_kept, 4 * p + blk - 1)
                pe.wait_ge(relu_dve, n + 1)
                pe.wait_ge(relu_act, n + 1)
                for j in range(4):
                    ins = mm(bank[SCORE[blk % 2]][32 * j:32 * j + 32, :], wsc[:, s, :],
                             relu_ring[:, n % RING, j].rearrange("p q k -> p (q k)"),
                             start=(s == 0), stop=(s == 7))
                ins.then_inc(score_mm, 1)

            def transpose_probs(p, blk):
                pe.wait_ge(exp_ready, 4 * p + blk + 1)
                if blk > 0:
                    pe.wait_ge(pt_ready, 4 * p + blk)
                elif p >= 1:
                    pe.wait_ge(out_ready, p)
                for kh in range(2):
                    for qi in range(2):
                        ins = nc.tensor.transpose(
                            bank[MISC][:, P * (2 * kh + qi):P * (2 * kh + qi + 1)],
                            sc_sb[:, p % 2, 2 * blk + qi, P * kh:P * (kh + 1)], ident[:])
                ins.then_inc(pt_mm, 1)

            def attend(p):
                pe.wait_ge(pt_ready, 4 * (p + 1))
                pe.wait_ge(v_ready, p + 1)
                for part in range(2):
                    for kh in range(2):
                        for bg_ in range(4):
                            b, gg = bg_ // 2, bg_ % 2
                            lhs = v_sb[:, p % 2, 2 * b + kh, gg, :] if part == 0 else ones32[:]
                            ins = mm(bank[MISC][32 * bg_:32 * bg_ + 32, L * part:L * (part + 1)], lhs,
                                     pt[:, kh, bg_].rearrange("p b q j -> p (b q j)"),
                                     start=(kh == 0), stop=(kh == 1))
                ins.then_inc(pv_mm, 1)

            def transpose_att(p):
                pe.wait_ge(att_ready, p + 1)
                for half in range(2):
                    ins = nc.tensor.transpose(bank[MISC][:, P * half:P * (half + 1)],
                                              att[:, P * half:P * (half + 1)], ident[:])
                ins.then_inc(att_t, 1)

            def transpose_xn2(p):
                pe.wait_ge(xn2_ready, p + 1)
                if p >= 1:
                    pe.wait_ge(prod_ready, 4 * p)
                transpose_pieces(bank[DOWNB], 1).then_inc(xf_mm, 1)

            def gate(p):
                pe.wait_ge(xf_ready, p + 1)
                pe.wait_ge(h2_ready, p + 1)
                for i in range(TT):
                    for n, (w, s) in enumerate(((wf_hi, 0), (wf_mid, 0), (wf_lh, 1))):
                        ins = mm(bank[MISC][:, E * i:E * (i + 1)], xf[:, s, P * i:P * (i + 1)],
                                 w[:, E * H:], start=(n == 0), stop=(n == 2))
                ins.then_inc(gate_mm, 1)

            def transpose_gates(p):
                pe.wait_ge(w_ready, p + 1)
                for i in range(TT):
                    ins = nc.tensor.transpose(bank[MISC][0:E, P * i:P * (i + 1)], wdense[:, i, :], ident[:])
                ins.then_inc(wt_mm, 1)

            def up(p, i):
                n = 16 * p + i
                if n >= 2:
                    pe.wait_ge(gelu_ready, n - 1)
                ep, r = i // 4, i % 4
                col = (2 * ep + r % 2) * H + (r // 2) * P
                for k, (w, s) in enumerate(((wf_hi, 0), (wf_mid, 0), (wf_lh, 1))):
                    ins = mm(bank[UPB[n % 2]][:], w[:, col:col + P], xf[:, s, :], start=(k == 0), stop=(k == 2))
                ins.then_inc(up_mm, 1)

            def down(p, ep):
                n = 4 * p + ep
                pe.wait_ge(gelu_ready, 4 * (n + 1))
                if n >= 1:
                    pe.wait_ge(prod_ready, n)
                for ht in range(HT):
                    for e2 in range(2):
                        ins = mm(bank[DOWNB][64 * e2:64 * e2 + 64, :], wd[:, 2 * ep + e2, ht, :],
                                 hid[:, (4 * n + 2 * ht + e2) % 8, :], start=(ht == 0), stop=(ht == HT - 1))
                ins.then_inc(down_mm, 1)

            def fold_experts(p):
                pe.wait_ge(acc_ready, 4 * (p + 1))
                pe.wait_ge(wt_ready, p + 1)
                for i in range(TT):
                    ins = mm(bank[MISC][:, D * i:D * (i + 1)], acc[:, P * i:P * (i + 1)], fold[:],
                             start=True, stop=True)
                ins.then_inc(fold_mm, 1)

            pe.wait_ge(sel_ready, 1)
            stack_inputs(0)
            pe.wait_ge(wpc_ready, 1)
            for j in range(3):
                ins = mm(bank[TOKB[1]][0:KX, 0:192], sel[:, 3 + j, :], w_pc[:, j, :], start=(j == 0), stop=(j == 2))
            ins.then_inc(ws_mm, 1)
            pe.wait_ge(ws_ready, 1)
            pe.wait_ge(consts_set, 1)
            for t in range(T):
                tok_step(0, t)
            token_out(0)
            pe.wait_ge(identb_ready, 1)
            transpose_xn1(0)
            pe.wait_ge(wa_ready, 1)
            project(0)
            pe.wait_ge(ld_att, 32)
            for p in range(PAIRS):
                for g in range(SLOTS):
                    if p >= 1:
                        if 6 <= g < 10:
                            transpose_probs(p - 1, g - 6)
                        if g == 11:
                            attend(p - 1)
                        if g == 13:
                            transpose_att(p - 1)
                        if g == 18:
                            transpose_xn2(p - 1)
                        if g == 20:
                            pe.wait_ge(wf_ready, 1)
                            gate(p - 1)
                        if g in (24, 26, 28, 30):
                            down(p - 1, (g - 24) // 2)
                        if 21 <= g < 29:
                            up(p - 1, 2 * (g - 21))
                            up(p - 1, 2 * (g - 21) + 1)
                        if g == 23:
                            transpose_gates(p - 1)
                    if p + 1 < PAIRS:
                        if g == 0:
                            stack_inputs(p + 1)
                        if g % 2 == 0 and 2 <= g < 2 + 2 * T:
                            tok_step(p + 1, (g - 2) // 2)
                        if g == 19:
                            token_out(p + 1)
                        if g == 26:
                            transpose_xn1(p + 1)
                        if g == 28:
                            project(p + 1)
                    if SLOTS * p + g >= 1:
                        scores(SLOTS * p + g - 1)
                if p >= 1:
                    fold_experts(p - 1)
            scores(SLOTS * PAIRS - 1)
            p = PAIRS - 1
            for blk in range(BLOCKS):
                transpose_probs(p, blk)
            attend(p)
            transpose_att(p)
            transpose_xn2(p)
            gate(p)
            for i in range(4):
                up(p, i)
            transpose_gates(p)
            for i in range(4, 8):
                up(p, i)
            for ep in range(E // 2):
                down(p, ep)
                if ep < 2:
                    for i in range(8 + 4 * ep, 12 + 4 * ep):
                        up(p, i)
            fold_experts(p)


def kernel(x, L0_tok_W1, L0_tok_b1, L0_tok_W2, L0_tok_b2, L0_tok_W3, L0_tok_b3, L0_tok_W4, L0_tok_b4,
           L0_attn_Wq, L0_attn_Wk, L0_attn_Wv, L0_attn_w_mlp, L0_attn_b_mlp, L0_ffn_Wg, L0_ffn_bg,
           L0_ffn_W1, L0_ffn_b1, L0_ffn_W2, L0_ffn_b2):
    import numpy as np
    import concourse.bacc as bacc
    from concourse.bass_utils import run_bass_kernel_spmd

    f = lambda a: np.asarray(a)
    x, W1, W2, W3, W4 = f(x), f(L0_tok_W1), f(L0_tok_W2), f(L0_tok_W3), f(L0_tok_W4)
    arrays = {}
    xt = x.transpose(1, 0, 2)
    x9 = np.ones((K9, B * L), np.float32)
    x9[0:4] = xt.reshape(DIN, -1)
    x9[4:8] = xt[:, :, ::-1].reshape(DIN, -1)
    arrays["x9"] = x9
    w9 = np.zeros((K9, 2, 192), np.float32)
    w9[0:4, 0, 0:64] = W1.T
    w9[4:8, 0, 64:128] = W1.T
    w9[0:4, 0, 128:192] = W3.T
    w9[8, 0, 0:64] = f(L0_tok_b1)
    w9[8, 0, 64:128] = f(L0_tok_b1)
    w9[8, 0, 128:192] = f(L0_tok_b3)
    w9[8, 1, 0:64] = f(L0_tok_b2)
    w9[8, 1, 64:128] = f(L0_tok_b2)
    w9[8, 1, 128:192] = f(L0_tok_b4)
    arrays["w9"] = w9
    sel9 = np.zeros((K9, 6, KX), np.float32)
    for i in range(3):
        for j in range(3):
            for r in range(8):
                sel9[r, i, 24 * i + 8 * j + r] = 1
                sel9[r, 3 + j, 24 * i + 8 * j + r] = 1
    for j in range(3):
        sel9[8, 0, 72 + j] = 1
        sel9[8, 3 + j, 72 + j] = 1
    arrays["sel9"] = sel9.reshape(K9, -1)
    tokw = np.zeros((P, 192), np.float32)
    tokw[0:64, 0:64] = W2.T
    tokw[64:128, 64:128] = W2.T
    tokw[0:64, 128:192] = W4.T
    tokw[64:128, 128:192] = W4.T
    arrays["tokw"] = tokw
    arrays["ident"] = np.eye(P, dtype=np.float32)
    arrays["fold"] = np.concatenate([np.eye(D, dtype=np.float32)] * 2)
    arrays["iota"] = np.tile(np.arange(E, dtype=np.float32), (P, 1))
    wv = f(L0_attn_Wv).reshape(DG, G, D).transpose(1, 0, 2).reshape(D, D)
    wa = np.concatenate([f(L0_attn_Wq).T, f(L0_attn_Wk).T, wv.T], 1)
    arrays["wa"] = np.concatenate([wa, wa])
    wf = np.concatenate([f(L0_ffn_W1).transpose(1, 0, 2).reshape(D, E * H), f(L0_ffn_Wg)], 1)
    arrays["wf"] = np.concatenate([wf, wf])
    arrays["wd"] = f(L0_ffn_W2).reshape(E, HT, P, D).transpose(2, 0, 1, 3)
    arrays["b1"] = f(L0_ffn_b1).reshape(E, HT, P).transpose(2, 0, 1).reshape(P, E * HT)
    arrays["b2"] = f(L0_ffn_b2).reshape(E // 2, 2, D).transpose(1, 2, 0).reshape(P, E // 2)
    arrays["bg"] = f(L0_ffn_bg)
    arrays["bm"] = f(L0_attn_b_mlp)
    wsc = np.zeros((P, 8, 32), np.float32)
    for r in range(4):
        for s in range(8):
            wsc[32 * r:32 * r + 32, s, 4 * s + r] = f(L0_attn_w_mlp)
    arrays["wsc"] = wsc

    nc = bacc.Bacc("TRN2", target_bir_lowering=False, num_devices=1)
    arrays = {f"in_{k}": np.ascontiguousarray(a) for k, a in arrays.items()}
    args = [nc.dram_tensor(k, a.shape, mybir.dt.from_np(a.dtype), kind="ExternalInput").ap()
            for k, a in arrays.items()]
    out = nc.dram_tensor("out", (PAIRS, P, TT, D), F32, kind="ExternalOutput").ap()
    gates = nc.dram_tensor("gates", (PAIRS, E, TOK), F32, kind="Internal").ap()
    build(nc, *args, gates, out)
    r = run_bass_kernel_spmd(nc, [arrays], core_ids=[0])
    got = r.results[0]["out"]
    return np.ascontiguousarray(got.transpose(0, 2, 1, 3)).reshape(B, L, D)
```

```python
from contextlib import ExitStack

import concourse.bass as bass
from concourse import mybir

ALU = mybir.AluOpType
ACT = mybir.ActivationFunctionType
F32 = mybir.dt.float32
BF16 = mybir.dt.bfloat16
U32 = mybir.dt.uint32
AX = mybir.AxisListType

B, DIN, L = 8, 4, 256
D, E, H = 64, 8, 256
G, DG = 2, 32
T = 8
EPS = 1e-5
P = 128
PAIRS = B // 2
TOK = 2 * L
TT = TOK // P
BLOCKS = 4
SLOTS = 32
RING = 6
LAG = 3
KR = 11
KX = 3 * 3 * 8 + 3 * 3
WX = 256
HT = H // P
EULER = 2.718281828459045

AT_STACK, AT_TOK, AT_TOKEN_OUT, AT_XA, AT_PROJECT = -31, -29, -13, -6, -4
AT_KEEP_SCORES = (12, 20, 28, 36)
AT_EXP, AT_PROBS, AT_ATTEND, AT_ATT_T, AT_RESID1 = 37, 38, 43, 45, 46
AT_XF, AT_GATE, AT_WEIGHTS, AT_GATES_T, AT_UP = 50, 52, 55, 56, 52
AT_DOWN, AT_WEIGH = (58, 63, 67, 71), (61, 64, 68, 72)
AT_FOLD = 74
FIRST, LAST = -31, SLOTS * (PAIRS - 1) + AT_FOLD + 2


def act_share(g):
    return (3,) if g % 3 == 1 else (2, 3)


def build(nc, xw, sel_d, tokw, ident_d, fold_d, iota_d, wa_d, wf_d, wd_d, b1_d, b2_d, bg_d, bm_d,
          wsc_d, gates_dram, out_d):
    with ExitStack() as ctx:
        def sb(name, shape, dt=F32):
            return ctx.enter_context(nc.sbuf_tensor(name, shape, dt))

        def sem(name):
            return ctx.enter_context(nc.semaphore(name))

        x_sb = sb("x_sb", [KR, WX + PAIRS * TOK])
        x_res = sb("x_res", [KR, WX + PAIRS * TOK])
        x_pc = sb("x_pc", [KR, 3, WX + PAIRS * TOK], BF16)
        sel_f = sb("sel_f", [KR, 6 * KX])
        sel = sb("sel", [KR, 6, KX], BF16)
        ws = sb("ws", [KX, WX], BF16)
        tokw_sb = sb("tokw_sb", [P, 2 * P])
        ident = sb("ident", [P, P])
        ident_b = sb("ident_b", [P, P], BF16)
        fold = sb("fold", [P, P])
        iota8 = sb("iota8", [P, E])
        wa_sb = sb("wa_sb", [P, 192])
        wa_res = sb("wa_res", [P, 192])
        wa_hi = sb("wa_hi", [P, 192], BF16)
        wa_mid = sb("wa_mid", [P, 192], BF16)
        wa_lh = sb("wa_lh", [P, 192], BF16)
        NF = E * H + E
        wf_sb = sb("wf_sb", [P, NF])
        wf_hi = sb("wf_hi", [P, NF], BF16)
        wf_mid = sb("wf_mid", [P, NF], BF16)
        wf_lh = sb("wf_lh", [P, NF], BF16)
        wd = sb("wd", [P, E, HT, D])
        b1 = sb("b1", [P, E * HT])
        b2 = sb("b2", [P, E // 2])
        bg = sb("bg", [P, E])
        bm = sb("bm", [P, 1])
        neg_bm = sb("neg_bm", [P, 1])
        wsc = sb("wsc", [P, 8, 32])
        ones32 = sb("ones32", [P, 32])
        neg_half = sb("neg_half", [P, TT])
        euler = sb("euler", [P, TT])

        xs = sb("xs", [KX, TOK], BF16)
        state = sb("state", [P, 2, L + 1])
        last = sb("last", [P, 2, L + 1])
        h1 = sb("h1", [P, 2, TT, D])
        stats = sb("stats", [P, 2, TT, 6])
        mv = sb("mv", [P, 2, TT, 2])
        rstd = sb("rstd", [P, 2, TT])
        xn = sb("xn", [P, 2, TT, D])
        xn_res = sb("xn_res", [P, 2, TT, D])
        xn_pc = sb("xn_pc", [P, 2, TT, 4, D], BF16)
        xa = sb("xa", [P, 2, TOK], BF16)
        q_sb = sb("q_sb", [P, 2, L])
        nk_sb = sb("nk_sb", [P, 2, L])
        v_sb = sb("v_sb", [P, 2, TT, G, DG])

        relu_ring = sb("relu_ring", [P, RING, 4, 2, L])
        sc_sb = sb("sc_sb", [P, 2 * BLOCKS, L])
        mx = sb("mx", [P, 2 * BLOCKS])
        nmx = sb("nmx", [P, 2 * BLOCKS])
        pt = sb("pt", [P, 2, 4, BLOCKS, 2, 32])
        rec = sb("rec", [P, L])
        att = sb("att", [P, L])
        h2 = sb("h2", [P, TT, D])

        xf = sb("xf", [P, 2, TOK], BF16)
        lg = sb("lg", [P, TT, E])
        top = sb("top", [P, TT, 8])
        topi = sb("topi", [P, TT, 8], U32)
        topf = sb("topf", [P, TT, 2])
        gap = sb("gap", [P, TT])
        egap = sb("egap", [P, TT])
        gden = sb("gden", [P, TT])
        gw = sb("gw", [P, TT, 2])
        oh = sb("oh", [P, 2, TT, E])
        wdense = sb("wdense", [P, TT, E])
        wt_sb = sb("wt_sb", [E, TOK])
        wbc = sb("wbc", [P, E // 2, TOK])
        hid = sb("hid", [P, 8, TOK])
        prod = sb("prod", [P, 2, TOK])
        acc = sb("acc", [P, TOK])
        o_sb = sb("o_sb", [P, TT, D])

        bank = [ctx.enter_context(nc.psum_tensor(f"bank{i}", [P, 512], F32)) for i in range(8)]
        SCORE, TOKB, UPB, DOWNB, MISC = (0, 1), (2, 3), (4, 5), 6, 7

        ld_x = sem("ld_x"); ld_tok = sem("ld_tok"); ld_cst = sem("ld_cst"); ld_wa = sem("ld_wa"); ld_att = sem("ld_att")
        ld_ffn = sem("ld_ffn")
        consts_set = sem("consts_set")
        sel_ready = sem("sel_ready"); ws_mm = sem("ws_mm")
        ws_ready = sem("ws_ready")
        xpc0_ready = sem("xpc0_ready"); xpc_ready = sem("xpc_ready"); rstd0_ready = sem("rstd0_ready")
        rstd3_ready = sem("rstd3_ready")
        wa_ready = sem("wa_ready"); wf_ready = sem("wf_ready"); identb_ready = sem("identb_ready")
        nbm_ready = sem("nbm_ready")
        xs_mm = sem("xs_mm"); xs_ready = sem("xs_ready")
        tok_mm = [sem("tok_mm0"), sem("tok_mm1")]
        tok_relu = [sem("tok_relu0"), sem("tok_relu1")]
        h1_mm = sem("h1_mm"); h1_ready = sem("h1_ready"); h1_stats = sem("h1_stats")
        xn1_ready = sem("xn1_ready"); xa_mm = sem("xa_mm"); xa_ready = sem("xa_ready")
        qk_mm = sem("qk_mm"); v_mm = sem("v_mm"); qk_ready = sem("qk_ready"); v_ready = sem("v_ready")
        relu_dve = sem("relu_dve"); relu_act = sem("relu_act"); score_mm = sem("score_mm")
        score_kept = sem("score_kept"); nmx_ready = sem("nmx_ready"); exp_ready = sem("exp_ready")
        pt_mm = sem("pt_mm"); pt_ready = sem("pt_ready"); pv_mm = sem("pv_mm")
        att_ready = sem("att_ready"); att_t = sem("att_t"); h2_ready = sem("h2_ready")
        h2_stats = sem("h2_stats"); xn2_ready = sem("xn2_ready"); xf_mm = sem("xf_mm")
        xf_ready = sem("xf_ready"); gate_mm = sem("gate_mm"); lg_ready = sem("lg_ready")
        gap_ready = sem("gap_ready"); egap_ready = sem("egap_ready"); w_ready = sem("w_ready")
        wt_mm = sem("wt_mm"); wt_ready = sem("wt_ready"); wbc_ready = sem("wbc_ready")
        up_mm = sem("up_mm"); gelu_ready = sem("gelu_ready"); down_mm = sem("down_mm")
        prod_ready = sem("prod_ready"); acc_ready = sem("acc_ready"); fold_mm = sem("fold_mm")
        gates_out = sem("gates_out"); out_ready = sem("out_ready"); out_stored = sem("out_stored")
        dve_step = sem("dve_step"); pool_step = sem("pool_step")

        block = ctx.enter_context(nc.Block())

        def chain(eng, step):
            count = [0]

            def link(ins):
                count[0] += 1
                ins.then_inc(step, 1)
                eng.wait_ge(step, count[0])
            return link

        def norm_split(vec, link, src, k):
            link(vec.tensor_tensor(xn[:, k], src, mv[:, k, :, 0:1].broadcast_to([P, TT, D]),
                                   ALU.subtract))
            link(vec.tensor_tensor(xn[:, k], xn[:, k],
                                   rstd[:, k, :, None].broadcast_to([P, TT, D]), ALU.mult))
            link(vec.tensor_copy(xn_pc[:, k, :, 0], xn[:, k]))
            vec.tensor_copy(xn_pc[:, k, :, 2], xn_pc[:, k, :, 0])
            link(vec.tensor_tensor(xn_res[:, k], xn[:, k], xn_pc[:, k, :, 0], ALU.subtract))
            link(vec.tensor_copy(xn_pc[:, k, :, 1], xn_res[:, k]))
            return vec.tensor_tensor(xn_pc[:, k, :, 3], xn_res[:, k], xn_pc[:, k, :, 1], ALU.subtract)

        @block.sync
        def _(sp):
            for dst, src in ((x_sb[:, 0:WX + TOK], xw[:, 0:WX + TOK]), (sel_f[:], sel_d)):
                sp.dma_start(dst, src).then_inc(ld_x, 16)
            for dst, src in ((tokw_sb[:], tokw), (x_sb[:, WX + TOK:], xw[:, WX + TOK:])):
                sp.dma_start(dst, src).then_inc(ld_tok, 16)
            for dst, src in ((wa_sb[:], wa_d), (ident[:], ident_d)):
                sp.dma_start(dst, src).then_inc(ld_wa, 16)
            for dst, src in ((wsc[:], wsc_d), (bm[:], bm_d.partition_broadcast(P))):
                sp.dma_start(dst, src).then_inc(ld_att, 16)
            for dst, src in ((wf_sb[:], wf_d), (wd[:], wd_d), (b1[:], b1_d), (b2[:], b2_d),
                             (bg[:], bg_d.partition_broadcast(P)), (fold[:], fold_d),
                             (iota8[:], iota_d)):
                sp.dma_start(dst, src).then_inc(ld_ffn, 16)
            for p in range(PAIRS):
                sp.wait_ge(wt_ready, p + 1)
                if p >= 1:
                    sp.wait_ge(prod_ready, 4 * p)
                sp.dma_start(gates_dram[p], wt_sb[:]).then_inc(gates_out, 16)
                sp.wait_ge(gates_out, 16 * (p + 1))
                for half in range(2):
                    sp.dma_start(wbc[64 * half:64 * half + 64],
                                 gates_dram[p].rearrange("(a h) t -> h a t", h=2)[half].partition_broadcast(64)
                                 ).then_inc(wbc_ready, 16)
                sp.wait_ge(out_ready, p + 1)
                sp.dma_start(out_d[p], o_sb[:]).then_inc(out_stored, 16)
            sp.wait_ge(out_stored, 16 * PAIRS)

        @block.gpsimd
        def _(pool):
            link = chain(pool, pool_step)
            vec = nc.gpsimd
            vec.memset(neg_half[:], -0.5)
            vec.memset(euler[:], EULER)
            vec.memset(ones32[:], 1.0)
            vec.memset(state[:, :, 0:1], 0.0)
            vec.memset(last[:], 0.0).then_inc(consts_set, 1)
            pool.wait_ge(consts_set, 1)

            def inv_std(k):
                link(vec.tensor_scalar(rstd[:, k], mv[:, k, :, 1], EPS, None, ALU.add))
                return vec.tensor_tensor(rstd[:, k], rstd[:, k], neg_half[:], ALU.pow)

            def norm1(p):
                pool.wait_ge(h1_stats, p + 1)
                link(inv_std(0))
                if p >= 1:
                    pool.wait_ge(xa_mm, p)
                norm_split(vec, link, h1[:, p % 2], 0).then_inc(xn1_ready, 1)

            def norm2(p):
                pool.wait_ge(h2_stats, p + 1)
                if p >= 1:
                    pool.wait_ge(xf_mm, p)
                if p == PAIRS - 1:
                    inv_std(1).then_inc(rstd3_ready, 1)
                else:
                    link(inv_std(1))
                    norm_split(vec, link, h2[:], 1).then_inc(xn2_ready, 1)

            def gate_exp(p):
                pool.wait_ge(gap_ready, p + 1)
                vec.tensor_tensor(egap[:], euler[:], gap[:], ALU.pow).then_inc(egap_ready, 1)

            def expert_sum(p, ep):
                pool.wait_ge(prod_ready, 4 * p + ep + 1)
                if ep == 0:
                    if p >= 1:
                        pool.wait_ge(fold_mm, p)
                    vec.tensor_copy(acc[:], prod[:, 0]).then_inc(acc_ready, 1)
                else:
                    pool.wait_ge(acc_ready, 4 * p + ep)
                    vec.tensor_tensor(acc[:], acc[:], prod[:, ep % 2],
                                      ALU.add).then_inc(acc_ready, 1)

            pool.wait_ge(ld_tok, 32)
            for p in range(1, PAIRS):
                if p == PAIRS - 1:
                    pool.wait_ge(h1_stats, 1)
                    inv_std(0).then_inc(rstd0_ready, 1)
                c = slice(WX + p * TOK, WX + (p + 1) * TOK)
                link(vec.tensor_copy(x_pc[:, 0, c], x_sb[:, c]))
                link(vec.tensor_tensor(x_res[:, c], x_sb[:, c], x_pc[:, 0, c], ALU.subtract))
                link(vec.tensor_copy(x_pc[:, 1, c], x_res[:, c]))
                vec.tensor_tensor(x_pc[:, 2, c], x_res[:, c], x_pc[:, 1, c],
                                  ALU.subtract).then_inc(xpc_ready, 1)
            pool.wait_ge(ld_ffn, 16 * 7)
            link(vec.tensor_copy(wf_hi[:], wf_sb[:]))
            link(vec.tensor_copy(wf_lh[64:128], wf_hi[64:128]))
            link(vec.tensor_tensor(wf_sb[:], wf_sb[:], wf_hi[:], ALU.subtract))
            link(vec.tensor_copy(wf_mid[:], wf_sb[:]))
            vec.tensor_tensor(wf_lh[0:64], wf_sb[0:64], wf_mid[0:64],
                              ALU.subtract).then_inc(wf_ready, 1)
            for n in range(FIRST, LAST):
                for p in range(PAIRS):
                    g = n - SLOTS * p
                    if g == AT_TOKEN_OUT + 3 and p >= 1:
                        norm1(p)
                    if g == AT_RESID1 + 1:
                        norm2(p)
                    if g == AT_GATE + 2:
                        gate_exp(p)
                    if g in AT_WEIGH:
                        expert_sum(p, AT_WEIGH.index(g))

        @block.scalar
        def _(act):
            def stack_inputs(p):
                act.wait_ge(xs_mm, p + 1)
                nc.scalar.copy(xs[:], bank[TOKB[0]][0:KX, :]).then_inc(xs_ready, 1)

            def tok_step(p, t):
                act.wait_ge(tok_mm[0], T * p + t + 1)
                src = bank[TOKB[0]]
                if t < T - 1:
                    nc.scalar.activation(state[:, 0, 1:L + 1], src[:, 0:L],
                                         ACT.Relu).then_inc(tok_relu[0], 1)
                else:
                    nc.scalar.activation(last[0:64, 0, 1:L], src[0:64, 0:L - 1],
                                         ACT.Relu).then_inc(tok_relu[0], 1)
                    nc.scalar.activation(last[64:128, 0, L - 2::-1], src[64:128, 0:L - 1],
                                         ACT.Relu).then_inc(tok_relu[0], 1)

            def token_out(p):
                act.wait_ge(h1_mm, p + 1)
                if p >= 2:
                    act.wait_ge(h2_ready, p - 1)
                nc.scalar.activation(h1[:, p % 2],
                                     bank[TOKB[0]][:].rearrange("p (t c) -> p t c", c=P)[:, :, 0:D], ACT.Relu
                                     ).then_inc(h1_ready, 1)

            def keep_qk(p):
                act.wait_ge(qk_mm, p + 1)
                if p >= 2:
                    act.wait_ge(relu_dve, SLOTS * (p - 1))
                src = bank[TOKB[0]]
                nc.scalar.copy(q_sb[:, p % 2, :], src[:, 0:L]).then_inc(qk_ready, 1)
                nc.scalar.mul(nk_sb[:, p % 2, :], src[:, L:2 * L], -1.0).then_inc(qk_ready, 1)

            def relu_tiles(n):
                p, g = n // SLOTS, n % SLOTS
                if n >= RING:
                    act.wait_ge(score_mm, n - RING + 1)
                for j in act_share(g):
                    for qi in range(2):
                        q = (g // 8) * 64 + qi * 32 + j * 8 + g % 8
                        ins = nc.scalar.activation(relu_ring[:, n % RING, j, qi, :], nk_sb[:, p % 2, :],
                                                   ACT.Relu, bias=q_sb[:, p % 2, q:q + 1])
                ins.then_inc(relu_act, 1)

            def exps(p):
                act.wait_ge(nmx_ready, p + 1)
                for blk in range(BLOCKS):
                    for qi in range(2):
                        c = 2 * blk + qi
                        ins = nc.scalar.activation(sc_sb[:, c, :], sc_sb[:, c, :], ACT.Exp,
                                                   bias=nmx[:, c:c + 1])
                    ins.then_inc(exp_ready, 1)

            def gelu(p, i):
                n = 16 * p + i
                act.wait_ge(up_mm, n + 1)
                if n >= 8:
                    act.wait_ge(down_mm, (n - 8) // 4 + 1)
                ep, r = i // 4, i % 4
                col = (2 * ep + r % 2) * HT + r // 2
                nc.scalar.activation(hid[:, n % 8, :], bank[UPB[n % 2]][:], ACT.Gelu,
                                     bias=b1[:, col:col + 1]).then_inc(gelu_ready, 1)

            def keep_wt(p):
                act.wait_ge(wt_mm, p + 1)
                if p >= 1:
                    act.wait_ge(gates_out, 16 * p)
                nc.scalar.copy(wt_sb[:], bank[MISC][0:E, :]).then_inc(wt_ready, 1)

            act.wait_ge(ws_mm, 1)
            nc.scalar.copy(ws[:], bank[TOKB[1]][0:KX, 0:WX]).then_inc(ws_ready, 1)
            for n in range(FIRST, LAST):
                for p in range(PAIRS):
                    g = n - SLOTS * p
                    if g == AT_STACK + 1:
                        stack_inputs(p)
                    if AT_TOK < g <= AT_TOK + 2 * T and (g - AT_TOK) % 2 == 1:
                        tok_step(p, (g - AT_TOK) // 2)
                    if g == AT_TOKEN_OUT + 1:
                        token_out(p)
                    if g == AT_PROJECT + 1:
                        keep_qk(p)
                    if g == 0:
                        act.wait_ge(qk_ready, 2 * (p + 1))
                    if g == AT_EXP:
                        exps(p)
                    if g == AT_UP and p == 0:
                        act.wait_ge(ld_ffn, 16 * 7)
                    if AT_UP < g <= AT_UP + 16:
                        gelu(p, g - AT_UP - 1)
                    if g == AT_GATES_T + 1:
                        keep_wt(p)
                if 0 <= n < SLOTS * PAIRS:
                    relu_tiles(n)

        @block.vector
        def _(dve):
            link = chain(dve, dve_step)
            vec = nc.vector

            def tok_step(p, t):
                dve.wait_ge(tok_mm[1], T * p + t + 1)
                src = bank[TOKB[1]]
                if t < T - 1:
                    vec.tensor_scalar(state[:, 1, 1:L + 1], src[:, 0:L], 0.0, None,
                                      ALU.max).then_inc(tok_relu[1], 1)
                else:
                    vec.tensor_scalar(last[0:64, 1, 1:L], src[0:64, 0:L - 1], 0.0, None,
                                      ALU.max).then_inc(tok_relu[1], 1)
                    vec.tensor_scalar(last[64:128, 1, L - 2::-1], src[64:128, 0:L - 1], 0.0, None,
                                      ALU.max).then_inc(tok_relu[1], 1)

            def token_stats(src, k):
                for i in range(TT):
                    ins = vec.bn_stats(stats[:, k, i, :], src[:, i, :])
                link(ins)
                for i in range(TT):
                    ins = vec.bn_aggr(mv[:, k, i, :], stats[:, k, i, :])
                return ins

            def stats1(p):
                dve.wait_ge(h1_ready, p + 1)
                if p >= 1:
                    dve.wait_ge(xn1_ready, p)
                token_stats(h1[:, p % 2], 0).then_inc(h1_stats, 1)

            def keep_xa(p):
                dve.wait_ge(xa_mm, p + 1)
                if p >= 1:
                    dve.wait_ge(v_mm, p)
                    dve.wait_ge(qk_mm, p)
                vec.tensor_copy(xa[:].rearrange("p a t -> p (a t)"), bank[TOKB[1]][:].bitcast(BF16)
                                ).then_inc(xa_ready, 1)

            def keep_v(p):
                dve.wait_ge(v_mm, p + 1)
                if p >= 2:
                    dve.wait_ge(pv_mm, p - 1)
                vec.tensor_copy(v_sb[:, p % 2].rearrange("p t g d -> p (t g d)"),
                                bank[TOKB[1]][:, 0:TT * D]).then_inc(v_ready, 1)

            def relu_tiles(n):
                p, g = n // SLOTS, n % SLOTS
                if n >= RING:
                    dve.wait_ge(score_mm, n - RING + 1)
                for j in range(4):
                    if j in act_share(g):
                        continue
                    for qi in range(2):
                        q = (g // 8) * 64 + qi * 32 + j * 8 + g % 8
                        ins = vec.tensor_scalar(relu_ring[:, n % RING, j, qi, :], nk_sb[:, p % 2, :],
                                                q_sb[:, p % 2, q:q + 1], 0.0, ALU.add, ALU.max)
                ins.then_inc(relu_dve, 1)

            def keep_scores(p, blk):
                dve.wait_ge(score_mm, SLOTS * p + 8 * (blk + 1))
                if p >= 1:
                    dve.wait_ge(pt_mm, 4 * (p - 1) + blk + 1)
                    dve.wait_ge(nmx_ready, p)
                for qi in range(2):
                    c = 2 * blk + qi
                    ins = vec.tensor_scalar(sc_sb[:, c, :],
                                            bank[SCORE[blk % 2]][:, qi * L:(qi + 1) * L],
                                            neg_bm[:, 0:1], None, ALU.max, ALU.max,
                                            accum_out=mx[:, c:c + 1])
                ins.then_inc(score_kept, 1)

            def neg_max(p):
                dve.wait_ge(score_kept, 4 * (p + 1))
                if p >= 1:
                    dve.wait_ge(exp_ready, 4 * p)
                vec.tensor_scalar(nmx[:], mx[:], -1.0, None, ALU.mult).then_inc(nmx_ready, 1)

            def keep_pt(p, blk):
                dve.wait_ge(pt_mm, 4 * p + blk + 1)
                if p >= 1 and blk == 0:
                    dve.wait_ge(pv_mm, p)
                for kh in range(2):
                    ins = vec.tensor_copy(
                        pt[:, kh, :, blk].rearrange("p b q j -> p q j b"),
                        bank[MISC][:, 256 * kh:256 * kh + 256].rearrange("p (q j b) -> p q j b", q=2, b=4))
                ins.then_inc(pt_ready, 1)

            def weigh(p):
                dve.wait_ge(pv_mm, p + 1)
                if p >= 1:
                    dve.wait_ge(att_t, p)
                link(vec.reciprocal(rec[:], bank[MISC][:, L:2 * L]))
                vec.tensor_tensor(att[:], bank[MISC][:, 0:L], rec[:], ALU.mult).then_inc(att_ready, 1)

            def residual1(p):
                dve.wait_ge(att_t, p + 1)
                if p >= 1:
                    dve.wait_ge(out_ready, p)
                for half in range(2):
                    src = bank[MISC][:, 128 * half:128 * half + 128].rearrange(
                        "p (b g d) -> p b g d", b=2, g=G)
                    old = h1[:, p % 2].rearrange("p (b h) (d g) -> p h b g d", h=2, g=G)[:, half]
                    new = h2[:].rearrange("p (b h) (d g) -> p h b g d", h=2, g=G)[:, half]
                    ins = vec.tensor_tensor(new, src, old, ALU.add)
                ins.then_inc(h2_ready, 1)
                dve.wait_ge(h2_ready, p + 1)
                token_stats(h2, 1).then_inc(h2_stats, 1)

            def keep_xf(p):
                dve.wait_ge(xf_mm, p + 1)
                if p >= 1:
                    dve.wait_ge(up_mm, 16 * p)
                vec.tensor_copy(xf[:].rearrange("p a t -> p (a t)"), bank[DOWNB][:].bitcast(BF16)
                                ).then_inc(xf_ready, 1)

            def top2(p):
                dve.wait_ge(gate_mm, p + 1)
                ins = vec.tensor_tensor(lg[:], bank[MISC][:, 0:TT * E].rearrange("p (t e) -> p t e", e=E),
                                        bg[:, None, :].broadcast_to([P, TT, E]), ALU.add)
                ins.then_inc(lg_ready, 1)
                dve.wait_ge(lg_ready, p + 1)
                for i in range(TT):
                    ins = vec.max(top[:, i, :], lg[:, i, :])
                link(ins)
                vec.tensor_tensor(gap[:], top[:, :, 1], top[:, :, 0], ALU.subtract
                                  ).then_inc(gap_ready, 1)
                for i in range(TT):
                    ins = vec.max_index(topi[:, i, :], top[:, i, :], lg[:, i, :])
                link(ins)
                link(vec.tensor_copy(topf[:], topi[:, :, 0:2]))
                for k in range(2):
                    ins = vec.tensor_tensor(oh[:, k], iota8[:, None, :].broadcast_to([P, TT, E]),
                                            topf[:, :, k:k + 1].broadcast_to([P, TT, E]), ALU.is_equal)
                link(ins)

            def gate_weights(p):
                dve.wait_ge(egap_ready, p + 1)
                link(vec.tensor_scalar(gden[:], egap[:], 1.0, None, ALU.add))
                link(vec.reciprocal(gw[:, :, 0], gden[:]))
                link(vec.tensor_tensor(gw[:, :, 1], gw[:, :, 0], egap[:], ALU.mult))
                for k in range(2):
                    ins = vec.tensor_tensor(oh[:, k], oh[:, k],
                                            gw[:, :, k:k + 1].broadcast_to([P, TT, E]), ALU.mult)
                link(ins)
                vec.tensor_tensor(wdense[:], oh[:, 0], oh[:, 1], ALU.add).then_inc(w_ready, 1)

            def weigh_expert(p, ep):
                n = 4 * p + ep
                dve.wait_ge(down_mm, n + 1)
                dve.wait_ge(wbc_ready, 32 * (p + 1))
                if n >= 2:
                    dve.wait_ge(acc_ready, n - 1)
                vec.scalar_tensor_tensor(prod[:, n % 2], bank[DOWNB][:], b2[:, ep:ep + 1], wbc[:, ep, :],
                                         ALU.add, ALU.mult).then_inc(prod_ready, 1)

            def residual2(p):
                dve.wait_ge(fold_mm, p + 1)
                if p >= 1:
                    dve.wait_ge(out_stored, 16 * p)
                vec.tensor_tensor(o_sb[:], bank[DOWNB][:].rearrange("p (t c) -> p t c", c=P)[:, :, 0:D],
                                  h2[:], ALU.add).then_inc(out_ready, 1)

            dve.wait_ge(ld_x, 32)
            vec.tensor_copy(sel[:].rearrange("k s n -> k (s n)"), sel_f[:]).then_inc(sel_ready, 1)
            c = slice(0, WX + TOK)
            link(vec.tensor_copy(x_pc[:, 0, c], x_sb[:, c]))
            link(vec.tensor_tensor(x_res[:, c], x_sb[:, c], x_pc[:, 0, c], ALU.subtract))
            link(vec.tensor_copy(x_pc[:, 1, c], x_res[:, c]))
            vec.tensor_tensor(x_pc[:, 2, c], x_res[:, c], x_pc[:, 1, c],
                              ALU.subtract).then_inc(xpc0_ready, 1)
            dve.wait_ge(ld_wa, 32)
            vec.tensor_copy(ident_b[:], ident[:]).then_inc(identb_ready, 1)
            link(vec.tensor_copy(wa_hi[:], wa_sb[:]))
            vec.tensor_copy(wa_lh[64:128], wa_hi[64:128])
            link(vec.tensor_tensor(wa_res[:], wa_sb[:], wa_hi[:], ALU.subtract))
            link(vec.tensor_copy(wa_mid[:], wa_res[:]))
            vec.tensor_tensor(wa_lh[0:64], wa_res[0:64], wa_mid[0:64], ALU.subtract
                              ).then_inc(wa_ready, 1)
            dve.wait_ge(ld_att, 32)
            link(vec.tensor_scalar(neg_bm[:], bm[:], -1.0, None, ALU.mult))
            dve.wait_ge(consts_set, 1)
            for n in range(FIRST, LAST):
                for p in range(PAIRS):
                    g = n - SLOTS * p
                    if AT_TOK < g <= AT_TOK + 2 * T and (g - AT_TOK) % 2 == 1:
                        tok_step(p, (g - AT_TOK) // 2)
                    if g == AT_TOKEN_OUT + 2:
                        stats1(p)
                        if p == 0:
                            dve.wait_ge(h1_stats, 1)
                            dve.wait_ge(rstd0_ready, 1)
                            norm_split(vec, link, h1[:, 0], 0).then_inc(xn1_ready, 1)
                    if g == AT_XA + 1:
                        keep_xa(p)
                    if g == AT_PROJECT + 1:
                        keep_v(p)
                    if g == 0:
                        dve.wait_ge(qk_ready, 2 * (p + 1))
                    if g in AT_KEEP_SCORES:
                        keep_scores(p, AT_KEEP_SCORES.index(g))
                    if g == AT_KEEP_SCORES[3]:
                        neg_max(p)
                    if AT_PROBS < g <= AT_PROBS + BLOCKS:
                        keep_pt(p, g - AT_PROBS - 1)
                    if g == AT_ATTEND + 1:
                        weigh(p)
                    if g == AT_RESID1:
                        residual1(p)
                        if p == PAIRS - 1:
                            dve.wait_ge(rstd3_ready, 1)
                            norm_split(vec, link, h2[:], 1).then_inc(xn2_ready, 1)
                    if g == AT_XF + 1:
                        keep_xf(p)
                    if g == AT_GATE + 1:
                        dve.wait_ge(ld_ffn, 16 * 7)
                        top2(p)
                    if g == AT_WEIGHTS:
                        gate_weights(p)
                    if g in AT_WEIGH:
                        weigh_expert(p, AT_WEIGH.index(g))
                    if g == AT_FOLD + 1:
                        residual2(p)
                if 0 <= n < SLOTS * PAIRS:
                    relu_tiles(n)

        @block.tensor
        def _(pe):
            mm = nc.tensor.matmul

            def stack_inputs(p):
                if p == 0:
                    pe.wait_ge(xpc0_ready, 1)
                else:
                    pe.wait_ge(xpc_ready, p)
                    pe.wait_ge(qk_ready, 2 * p)
                for i in range(3):
                    ins = mm(bank[TOKB[0]][0:KX, :], sel[:, i, :], x_pc[:, i, WX + p * TOK:WX + (p + 1) * TOK],
                             start=(i == 0), stop=(i == 2))
                ins.then_inc(xs_mm, 1)

            def tok_step(p, t):
                for b in range(2):
                    if t == 0:
                        if b == 0:
                            pe.wait_ge(xs_ready, p + 1)
                        elif p >= 1:
                            pe.wait_ge(v_ready, p)
                    else:
                        pe.wait_ge(tok_relu[b], (T + 1) * p + t)
                    dst = bank[TOKB[b]][:, 0:L]
                    if t > 0:
                        mm(dst, tokw_sb[:, 0:P], state[:, b, 0:L], start=True, stop=False)
                    mm(dst, ws[:, 0:P], xs[:, b * L:(b + 1) * L], start=(t == 0),
                       stop=True).then_inc(tok_mm[b], 1)

            def token_out(p):
                for b in range(2):
                    pe.wait_ge(tok_relu[b], (T + 1) * (p + 1))
                for b in range(2):
                    for h in range(2):
                        dst = bank[TOKB[0]][:, P * (2 * b + h):P * (2 * b + h + 1)]
                        mm(dst, last[:, b, P * h:P * (h + 1)], tokw_sb[:, P:2 * P], start=True, stop=False)
                        ins = mm(dst, xs[:, b * L + P * h:b * L + P * (h + 1)], ws[:, P:2 * P],
                                 start=False, stop=True)
                ins.then_inc(h1_mm, 1)

            def transpose_pieces(dst, k):
                view = dst[:].bitcast(BF16)
                for s in range(2):
                    for i in range(TT):
                        ins = nc.tensor.transpose(view[:, 512 * s + P * i:512 * s + P * (i + 1)],
                                                  xn_pc[:, k, i, 2 * s:2 * s + 2, :].rearrange("p a d -> p (a d)"),
                                                  ident_b[:])
                return ins

            def transpose_xn1(p):
                pe.wait_ge(xn1_ready, p + 1)
                transpose_pieces(bank[TOKB[1]], 0).then_inc(xa_mm, 1)

            def project(p):
                pe.wait_ge(xa_ready, p + 1)
                pe.wait_ge(h1_ready, p + 1)
                terms = ((wa_hi, 0), (wa_mid, 0), (wa_lh, 1))
                for c in range(2):
                    for n, (w, s) in enumerate(terms):
                        for b in range(2):
                            ins = mm(bank[TOKB[0]][64 * b:64 * b + 64, L * c:L * (c + 1)],
                                     w[:, D * c:D * (c + 1)], xa[:, s, L * b:L * (b + 1)],
                                     start=(n == 0), stop=(n == 2))
                ins.then_inc(qk_mm, 1)
                for i in range(TT):
                    for n, (w, s) in enumerate(terms):
                        ins = mm(bank[TOKB[1]][:, D * i:D * (i + 1)], xa[:, s, P * i:P * (i + 1)],
                                 w[:, 2 * D:3 * D], start=(n == 0), stop=(n == 2))
                ins.then_inc(v_mm, 1)

            def scores(n):
                p, g = n // SLOTS, n % SLOTS
                blk, s = g // 8, g % 8
                if s == 0 and 4 * p + blk >= 2:
                    pe.wait_ge(score_kept, 4 * p + blk - 1)
                pe.wait_ge(relu_dve, n + 1)
                pe.wait_ge(relu_act, n + 1)
                for j in range(4):
                    ins = mm(bank[SCORE[blk % 2]][32 * j:32 * j + 32, :], wsc[:, s, :],
                             relu_ring[:, n % RING, j].rearrange("p q k -> p (q k)"),
                             start=(s == 0), stop=(s == 7))
                ins.then_inc(score_mm, 1)

            def transpose_probs(p, blk):
                pe.wait_ge(exp_ready, 4 * p + blk + 1)
                if blk > 0:
                    pe.wait_ge(pt_ready, 4 * p + blk)
                elif p >= 1:
                    pe.wait_ge(wt_ready, p)
                for kh in range(2):
                    for qi in range(2):
                        ins = nc.tensor.transpose(
                            bank[MISC][:, P * (2 * kh + qi):P * (2 * kh + qi + 1)],
                            sc_sb[:, 2 * blk + qi, P * kh:P * (kh + 1)], ident[:])
                ins.then_inc(pt_mm, 1)

            def attend(p):
                pe.wait_ge(pt_ready, 4 * (p + 1))
                pe.wait_ge(v_ready, p + 1)
                for part in range(2):
                    for kh in range(2):
                        for bg_ in range(4):
                            b, gg = bg_ // 2, bg_ % 2
                            lhs = v_sb[:, p % 2, 2 * b + kh, gg, :] if part == 0 else ones32[:]
                            ins = mm(bank[MISC][32 * bg_:32 * bg_ + 32, L * part:L * (part + 1)], lhs,
                                     pt[:, kh, bg_].rearrange("p b q j -> p (b q j)"),
                                     start=(kh == 0), stop=(kh == 1))
                ins.then_inc(pv_mm, 1)

            def transpose_att(p):
                pe.wait_ge(att_ready, p + 1)
                for half in range(2):
                    ins = nc.tensor.transpose(bank[MISC][:, P * half:P * (half + 1)],
                                              att[:, P * half:P * (half + 1)], ident[:])
                ins.then_inc(att_t, 1)

            def transpose_xn2(p):
                pe.wait_ge(xn2_ready, p + 1)
                if p >= 1:
                    pe.wait_ge(out_ready, p)
                transpose_pieces(bank[DOWNB], 1).then_inc(xf_mm, 1)

            def gate(p):
                pe.wait_ge(xf_ready, p + 1)
                pe.wait_ge(h2_ready, p + 1)
                for i in range(TT):
                    for n, (w, s) in enumerate(((wf_hi, 0), (wf_mid, 0), (wf_lh, 1))):
                        ins = mm(bank[MISC][:, E * i:E * (i + 1)], xf[:, s, P * i:P * (i + 1)],
                                 w[:, E * H:], start=(n == 0), stop=(n == 2))
                ins.then_inc(gate_mm, 1)

            def transpose_gates(p):
                pe.wait_ge(w_ready, p + 1)
                for i in range(TT):
                    ins = nc.tensor.transpose(bank[MISC][0:E, P * i:P * (i + 1)], wdense[:, i, :], ident[:])
                ins.then_inc(wt_mm, 1)

            def up(p, i):
                n = 16 * p + i
                if n >= 2:
                    pe.wait_ge(gelu_ready, n - 1)
                ep, r = i // 4, i % 4
                col = (2 * ep + r % 2) * H + (r // 2) * P
                for k, (w, s) in enumerate(((wf_hi, 0), (wf_mid, 0), (wf_lh, 1))):
                    ins = mm(bank[UPB[n % 2]][:], w[:, col:col + P], xf[:, s, :], start=(k == 0), stop=(k == 2))
                ins.then_inc(up_mm, 1)

            def down(p, ep):
                n = 4 * p + ep
                pe.wait_ge(gelu_ready, 4 * (n + 1))
                if n >= 1:
                    pe.wait_ge(prod_ready, n)
                for ht in range(HT):
                    for e2 in range(2):
                        ins = mm(bank[DOWNB][64 * e2:64 * e2 + 64, :], wd[:, 2 * ep + e2, ht, :],
                                 hid[:, (4 * n + 2 * ht + e2) % 8, :], start=(ht == 0), stop=(ht == HT - 1))
                ins.then_inc(down_mm, 1)

            def fold_experts(p):
                pe.wait_ge(acc_ready, 4 * (p + 1))
                for i in range(TT):
                    ins = mm(bank[DOWNB][:, P * i:P * (i + 1)], acc[:, P * i:P * (i + 1)], fold[:],
                             start=True, stop=True)
                ins.then_inc(fold_mm, 1)

            pe.wait_ge(sel_ready, 1)
            pe.wait_ge(xpc0_ready, 1)
            for j in range(3):
                ins = mm(bank[TOKB[1]][0:KX, 0:WX], sel[:, 3 + j, :], x_pc[:, j, 0:WX], start=(j == 0), stop=(j == 2))
            ins.then_inc(ws_mm, 1)
            for n in range(FIRST, LAST):
                for p in range(PAIRS):
                    g = n - SLOTS * p
                    if g == AT_STACK:
                        stack_inputs(p)
                        if p == 0:
                            pe.wait_ge(ws_ready, 1)
                            pe.wait_ge(ld_tok, 32)
                            pe.wait_ge(consts_set, 1)
                    if AT_TOK <= g < AT_TOK + 2 * T and (g - AT_TOK) % 2 == 0:
                        tok_step(p, (g - AT_TOK) // 2)
                    if g == AT_TOKEN_OUT:
                        token_out(p)
                    if g == AT_XA:
                        if p == 0:
                            pe.wait_ge(identb_ready, 1)
                        transpose_xn1(p)
                    if g == AT_PROJECT:
                        if p == 0:
                            pe.wait_ge(wa_ready, 1)
                        project(p)
                        if p == 0:
                            pe.wait_ge(ld_att, 32)
                    if AT_PROBS <= g < AT_PROBS + BLOCKS:
                        transpose_probs(p, g - AT_PROBS)
                    if g == AT_ATTEND:
                        attend(p)
                    if g == AT_ATT_T:
                        transpose_att(p)
                    if g == AT_XF:
                        transpose_xn2(p)
                    if g == AT_GATE:
                        if p == 0:
                            pe.wait_ge(wf_ready, 1)
                        gate(p)
                    if g in AT_DOWN:
                        down(p, AT_DOWN.index(g))
                    if AT_UP <= g < AT_UP + 16:
                        up(p, g - AT_UP)
                    if g == AT_GATES_T:
                        transpose_gates(p)
                    if g == AT_FOLD:
                        fold_experts(p)
                if 0 <= n - LAG < SLOTS * PAIRS:
                    scores(n - LAG)


def kernel(x, L0_tok_W1, L0_tok_b1, L0_tok_W2, L0_tok_b2, L0_tok_W3, L0_tok_b3, L0_tok_W4, L0_tok_b4,
           L0_attn_Wq, L0_attn_Wk, L0_attn_Wv, L0_attn_w_mlp, L0_attn_b_mlp, L0_ffn_Wg, L0_ffn_bg,
           L0_ffn_W1, L0_ffn_b1, L0_ffn_W2, L0_ffn_b2):
    import numpy as np
    import concourse.bacc as bacc
    from concourse.bass_utils import run_bass_kernel_spmd

    f = lambda a: np.asarray(a)
    x, W1, W2, W3, W4 = f(x), f(L0_tok_W1), f(L0_tok_W2), f(L0_tok_W3), f(L0_tok_W4)
    arrays = {}
    xt = x.transpose(1, 0, 2)
    xw = np.zeros((KR, WX + B * L), np.float32)
    xw[0:4, WX:] = xt.reshape(DIN, -1)
    xw[4:8, WX:] = xt[:, :, ::-1].reshape(DIN, -1)
    xw[8:, WX:] = 1
    xw[0:4, 0:64] = W1.T
    xw[4:8, 64:128] = W1.T
    for at in (0, 64):
        xw[0:4, 128 + at:192 + at] = W3.T
        xw[8, at:at + 64] = f(L0_tok_b1)
        xw[9, at:at + 64] = f(L0_tok_b2)
        xw[8, 128 + at:192 + at] = f(L0_tok_b3)
        xw[9:11, 128 + at:192 + at] = f(L0_tok_b4)
    arrays["xw"] = xw
    sel = np.zeros((KR, 6, KX), np.float32)
    for j in range(3):
        for i in range(3):
            for r in range(8):
                sel[r, i, 24 * i + 8 * j + r] = 1
                sel[r, 3 + j, 24 * i + 8 * j + r] = 1
        for r in range(3):
            sel[8 + r, 0, 72 + 3 * j + r] = 1
            sel[8 + r, 3 + j, 72 + 3 * j + r] = 1
    arrays["sel"] = sel.reshape(KR, -1)
    tokw = np.zeros((P, 2 * P), np.float32)
    tokw[0:64, 0:64] = W2.T
    tokw[64:128, 64:128] = W2.T
    for r in (0, 64):
        for c in (128, 192):
            tokw[r:r + 64, c:c + 64] = W4.T
    arrays["tokw"] = tokw
    arrays["ident"] = np.eye(P, dtype=np.float32)
    arrays["fold"] = np.tile(np.eye(D, dtype=np.float32), (2, 2))
    arrays["iota"] = np.tile(np.arange(E, dtype=np.float32), (P, 1))
    wv = f(L0_attn_Wv).reshape(DG, G, D).transpose(1, 0, 2).reshape(D, D)
    wa = np.concatenate([f(L0_attn_Wq).T, f(L0_attn_Wk).T, wv.T], 1)
    arrays["wa"] = np.concatenate([wa, wa])
    wf = np.concatenate([f(L0_ffn_W1).transpose(1, 0, 2).reshape(D, E * H), f(L0_ffn_Wg)], 1)
    arrays["wf"] = np.concatenate([wf, wf])
    arrays["wd"] = f(L0_ffn_W2).reshape(E, HT, P, D).transpose(2, 0, 1, 3)
    arrays["b1"] = f(L0_ffn_b1).reshape(E, HT, P).transpose(2, 0, 1).reshape(P, E * HT)
    arrays["b2"] = f(L0_ffn_b2).reshape(E // 2, 2, D).transpose(1, 2, 0).reshape(P, E // 2)
    arrays["bg"] = f(L0_ffn_bg)
    arrays["bm"] = f(L0_attn_b_mlp)
    wsc = np.zeros((P, 8, 32), np.float32)
    for r in range(4):
        for s in range(8):
            wsc[32 * r:32 * r + 32, s, 4 * s + r] = f(L0_attn_w_mlp)
    arrays["wsc"] = wsc

    nc = bacc.Bacc("TRN2", target_bir_lowering=False, num_devices=1)
    arrays = {f"in_{k}": np.ascontiguousarray(a) for k, a in arrays.items()}
    args = [nc.dram_tensor(k, a.shape, mybir.dt.from_np(a.dtype), kind="ExternalInput").ap()
            for k, a in arrays.items()]
    out = nc.dram_tensor("out", (PAIRS, P, TT, D), F32, kind="ExternalOutput").ap()
    gates = nc.dram_tensor("gates", (PAIRS, E, TOK), F32, kind="Internal").ap()
    build(nc, *args, gates, out)
    r = run_bass_kernel_spmd(nc, [arrays], core_ids=[0])
    got = r.results[0]["out"]
    return np.ascontiguousarray(got.transpose(0, 2, 1, 3)).reshape(B, L, D)
```

```python
from contextlib import ExitStack

from concourse import mybir

ALU = mybir.AluOpType
ACT = mybir.ActivationFunctionType
F32 = mybir.dt.float32
BF16 = mybir.dt.bfloat16
U32 = mybir.dt.uint32

B, DIN, L = 8, 4, 256
D, E, H = 64, 8, 256
G, DG = 2, 32
T = 8
EPS = 1e-5
P = 128
PAIRS = B // 2
TOK = 2 * L
TT = TOK // P
BLOCKS = 4
SLOTS = 32
KEYS_FROM = 3
RING = 6
LAG = 3
KR = 11
KX = 3 * 3 * 8 + 3 * 3
WX = 256
GROUPS = 3
HT = H // P
EULER = 2.718281828459045

TOKEN_AT = [
    dict(
        pe_stack=(-34,), pe_step=(-29, -27, -23, -23, -21, -18, -17, -15), pe_out=(-11,), pe_xa=(-4,),
        pe_project=(-4,), act_stack=(-32,), act_step=(-29, -27, -27, -23, -20, -17, -16, -11), act_out=(-8,),
        act_qk=(-1,), dve_step=(-29, -27, -24, -22, -19, -16, -16, -14), dve_stats=(-6,), dve_xa=(-6,),
        dve_v=(2,), pool_norm=(-3,), pe_values=(-2,), pe_keys=(1,)),
    dict(
        pe_stack=(-55,), pe_step=(-52, -49, -49, -47, -47, -47, -43, -38), pe_out=(-35,), pe_xa=(-14,),
        pe_project=(-13,), act_stack=(-55,), act_step=(-51, -49, -46, -45, -41, -41, -39, -37), act_out=(-31,),
        act_qk=(-2,), dve_step=(-50, -48, -47, -47, -46, -42, -39, -37), dve_stats=(-27,), dve_xa=(-11,),
        dve_v=(-2,), pool_norm=(-19,), pool_inputs=(-42,), pe_values=(-4,), pe_keys=(0,)),
    dict(
        pe_stack=(-61,), pe_step=(-60, -59, -57, -56, -53, -52, -51, -47), pe_out=(-46,), pe_xa=(-38,),
        pe_project=(-35,), act_stack=(-60,), act_step=(-58, -56, -55, -52, -51, -50, -48, -46), act_out=(-45,),
        act_qk=(-34,), dve_step=(-58, -58, -57, -56, -52, -50, -48, -45), dve_stats=(-43,), dve_xa=(-36,),
        dve_v=(-33,), pool_norm=(-50,), pe_values=(-34,), pe_keys=(2,)),
    dict(
        pe_stack=(-65,), pe_step=(-61, -59, -57, -54, -51, -48, -43, -42), act_stack=(-61,),
        act_step=(-60, -59, -56, -53, -50, -45, -44, -40), dve_step=(-62, -59, -56, -53, -50, -45, -44, -39),
        pe_out=(-39,), act_out=(-39,), dve_stats=(-39,), pool_norm=(-40,), pe_xa=(-28,), dve_xa=(-27,),
        pe_project=(-25,), act_qk=(-23,), pe_values=(-15,), dve_v=(-8,), pe_keys=(0,))]
FFN_PIECES_AT = 19
FREED = {2: 1, 3: 3}
WARM_UP, WARM_STACK, WARM_STEP = 17, 3, 1
KEEP_AT = [(18, 25, 29, 34), (17, 24, 32, 36), (14, 25, 25, 35), (18, 18, 37, 37)]
ACT_TILES = [
    (2, 1, 1, 7, 2, 5, 2, 3, 4, 5, 4, 3, 5, 5, 5, 3, 4, 7, 3, 3, 5, 3, 2, 7, 4, 5, 1, 5, 2, 1, 5, 1),
    (3, 1, 4, 5, 4, 3, 7, 5, 6, 5, 2, 4, 6, 5, 3, 1, 3, 6, 3, 4, 1, 6, 1, 2, 1, 2, 1, 4, 3, 2, 5, 6),
    (2, 1, 3, 2, 1, 4, 7, 1, 3, 7, 2, 2, 5, 4, 5, 1, 3, 4, 4, 2, 5, 4, 2, 2, 1, 2, 1, 4, 4, 1, 1, 3),
    (5, 5, 2, 2, 3, 2, 7, 3, 2, 3, 6, 4, 7, 6, 3, 7, 1, 5, 3, 1, 3, 5, 4, 3, 3, 2, 6, 2, 3, 5, 1, 3)]
UNIT_AT = [
    dict(
        pe_probs=(39, 40, 41, 42), pe_attend=(43,), pe_att_t=(45,), pe_xf=(53,), pe_gate=(54,),
        pe_gates_t=(58,), pe_up=(54, 54, 55, 57, 57, 59, 59, 60, 60, 61, 66, 66, 67, 67, 68, 72),
        pe_down=(59, 66, 69, 73), pe_fold=(80,), act_exp=(37, 37, 38, 38),
        act_gelu=(54, 55, 56, 57, 58, 60, 60, 60, 61, 63, 67, 67, 67, 68, 69, 70), act_wt=(59,), dve_neg=(35,),
        dve_pt=(40, 41, 41, 43), dve_weigh=(46,), dve_resid=(46,), dve_xf=(52,), dve_top=(53,),
        dve_gates=(56,), dve_prod=(62, 68, 71, 76), dve_out=(82,), pool_norm=(48,), pool_exp=(54,),
        pool_sum=(59, 59, 69, 73)),
    dict(
        pe_probs=(37, 38, 39, 40), pe_attend=(41,), pe_att_t=(44,), pe_xf=(52,), pe_gate=(54,),
        pe_gates_t=(55,), pe_up=(54, 54, 55, 55, 55, 59, 59, 60, 60, 61, 63, 64, 65, 66, 66, 67),
        pe_down=(59, 64, 67, 68), pe_fold=(73,), act_exp=(37, 37, 37, 37),
        act_gelu=(53, 54, 54, 54, 59, 59, 60, 60, 61, 61, 65, 65, 66, 66, 67, 68), act_wt=(56,), dve_neg=(37,),
        dve_pt=(38, 39, 40, 42), dve_weigh=(44,), dve_resid=(45,), dve_xf=(51,), dve_top=(52,),
        dve_gates=(53,), dve_prod=(60, 63, 68, 70), dve_out=(75,), pool_norm=(51,), pool_exp=(51,),
        pool_sum=(62, 66, 74, 74)),
    dict(
        pe_probs=(37, 40, 41, 41), pe_attend=(42,), pe_att_t=(43,), pe_xf=(52,), pe_gate=(52,),
        pe_gates_t=(58,), pe_up=(52, 53, 53, 55, 55, 58, 58, 59, 60, 60, 61, 63, 63, 64, 64, 66),
        pe_down=(59, 63, 67, 70), pe_fold=(75,), act_exp=(37, 39, 40, 41),
        act_gelu=(53, 53, 54, 57, 58, 58, 59, 60, 61, 61, 61, 62, 62, 65, 65, 66), act_wt=(58,), dve_neg=(36,),
        dve_pt=(39, 40, 41, 41), dve_weigh=(43,), dve_resid=(44,), dve_xf=(51,), dve_top=(53,),
        dve_gates=(56,), dve_prod=(61, 67, 69, 72), dve_out=(79,), pool_norm=(50,), pool_exp=(52,),
        pool_sum=(71, 71, 72, 75)),
    dict(
        pe_probs=(20, 21), pe_attend=(24,), pe_att_t=(28,), pe_xf=(33,), pe_gate=(34,), pe_gates_t=(35,),
        pe_up=(34, 35, 37, 37, 38, 38, 39, 39, 40, 40, 42, 43, 43, 44, 45, 45), pe_down=(41, 43, 45, 46),
        pe_fold=(52,), act_exp=(20, 20),
        act_gelu=(36, 37, 38, 38, 39, 39, 40, 40, 42, 42, 43, 44, 44, 44, 45, 45), act_wt=(37,), dve_neg=(18,),
        dve_pt=(20, 23), dve_weigh=(28,), dve_resid=(30,), dve_xf=(34,), dve_top=(35,), dve_gates=(36,),
        dve_prod=(42, 43, 46, 47), dve_out=(62,), pool_norm=(25,), pool_exp=(29,), pool_sum=(44, 47, 50, 58)),
    dict(
        pe_probs=(38, 38), pe_attend=(39,), pe_att_t=(41,), pe_xf=(44,), pe_gate=(45,), pe_gates_t=(47,),
        pe_up=(45, 45, 46, 46, 46, 46, 46, 46, 46, 46, 53, 57, 57, 57, 69, 69), pe_down=(48, 57, 70, 73),
        pe_fold=(69, 76, 76, 77), act_exp=(38, 38),
        act_gelu=(45, 45, 45, 45, 46, 46, 46, 53, 57, 57, 57, 57, 70, 70, 70, 70), act_wt=(50,), dve_neg=(37,),
        dve_pt=(37, 41), dve_weigh=(41,), dve_resid=(42,), dve_xf=(44,), dve_top=(46,), dve_gates=(49,),
        dve_prod=(69, 69, 74, 81), dve_out=(82,), pool_norm=(43,), pool_exp=(48,))]


class Unit:

    def __init__(self, pair, halves, at, misc, xf_bank, fold_bank):
        self.pair, self.halves, self.at = pair, halves, at
        self.blocks = range(2 * halves[0], 2 * halves[-1] + 2)
        self.tiles = [2 * b + h for b in range(2) for h in halves]
        self.tok = P * len(self.tiles)
        self.gate_cols = slice(2 * P * halves[0], 2 * P * halves[-1] + 2 * P)
        self.queries = slice(P * halves[0], P * halves[-1] + P)
        self.misc, self.xf_bank, self.fold_bank = misc, xf_bank, fold_bank


UNITS = [Unit(p, (0, 1), UNIT_AT[p], 7, 6, 2 if p == PAIRS - 2 else 6) for p in range(PAIRS - 1)]
UNITS += [Unit(PAIRS - 1, (0,), UNIT_AT[3], 2, 3, 2), Unit(PAIRS - 1, (1,), UNIT_AT[4], 7, 3, None)]
FIRST = min(SLOTS * p + slot for p, at in enumerate(TOKEN_AT) for slots in at.values() for slot in slots)
LAST = SLOTS * (PAIRS - 1) + max(slot for slots in UNIT_AT[-1].values() for slot in slots) + 1


def due(n, pair, at, step):
    return [i for i, slot in enumerate(at.get(step, ())) if SLOTS * pair + slot == n]


def build(nc, xw, sel_d, tokw, ident_d, fold_d, iota_d, wa_d, wf_d, wd_d, b1_d, b2_d, bg_d, bm_d,
          wsc_d, gates_dram, out_d):
    with ExitStack() as ctx:
        def sb(name, shape, dt=F32):
            return ctx.enter_context(nc.sbuf_tensor(name, shape, dt))

        def sem(name):
            return ctx.enter_context(nc.semaphore(name))

        x_sb = sb("x_sb", [32 * GROUPS, 3, L])
        x_pc = sb("x_pc", [32 * GROUPS, 3, 3, L], BF16)
        sel_f = sb("sel_f", [32 * GROUPS, 6 * KX])
        sel = sb("sel", [32 * GROUPS, 6, KX], BF16)
        ws = sb("ws", [KX, WX], BF16)
        tokw_sb = sb("tokw_sb", [P, 2 * P])
        ident = sb("ident", [P, P])
        ident_b = sb("ident_b", [P, P], BF16)
        fold = sb("fold", [P, P])
        iota8 = sb("iota8", [P, E])
        wa_sb = sb("wa_sb", [P, 192])
        wa_hi = sb("wa_hi", [P, 192], BF16)
        wa_mid = sb("wa_mid", [P, 192], BF16)
        wa_lh = sb("wa_lh", [P, 192], BF16)
        NF = E * H + E
        wf_sb = sb("wf_sb", [P, NF])
        wf_hi = sb("wf_hi", [P, NF], BF16)
        wf_mid = sb("wf_mid", [P, NF], BF16)
        wf_lh = sb("wf_lh", [P, NF], BF16)
        wd = sb("wd", [P, E, HT, D])
        b1 = sb("b1", [P, E * HT])
        b2 = sb("b2", [P, E // 2])
        bg = sb("bg", [P, E])
        bm = sb("bm", [P, 1])
        neg_bm = sb("neg_bm", [P, 1])
        wsc = sb("wsc", [P, 8, 32])
        ones32 = sb("ones32", [P, 32])
        neg_half = sb("neg_half", [P, TT])
        euler = sb("euler", [P, TT])

        zeros = sb("zeros", [P, TOK], BF16)

        xs = sb("xs", [KX, 2, TOK], BF16)
        state = sb("state", [P, 2, 2, L + 1])
        last = sb("last", [P, 2, 2, L + 1])
        h1 = sb("h1", [P, 3, TT, D])
        stats = sb("stats", [P, 2, TT, 6])
        mv = sb("mv", [P, 2, TT, 2])
        rstd = sb("rstd", [P, 2, TT])
        xn = sb("xn", [P, 2, TT, D])
        xn_res = sb("xn_res", [P, 2, TT, D])
        xn_pc = sb("xn_pc", [P, 2, TT, 4, D], BF16)
        xa = sb("xa", [P, 2, 2, TOK], BF16)
        q_sb = sb("q_sb", [P, 3, L])
        nk_sb = sb("nk_sb", [P, 3, L])
        v_sb = sb("v_sb", [P, 3, TT, G, DG])

        relu_ring = sb("relu_ring", [P, RING, 4, 2, L])
        sc_sb = sb("sc_sb", [P, 2 * BLOCKS, L])
        mx = sb("mx", [P, 2 * BLOCKS])
        nmx = sb("nmx", [P, 2 * BLOCKS])
        pt = sb("pt", [P, 2, 4, BLOCKS, 2, 32])
        rec = sb("rec", [P, L])
        att = sb("att", [P, L])
        h2 = sb("h2", [P, 2, TT, D])

        xf = sb("xf", [P, 2, 2, TOK], BF16)
        lg = sb("lg", [P, TT, E])
        top = sb("top", [P, TT, 8])
        topi = sb("topi", [P, TT, 8], U32)
        topf = sb("topf", [P, TT, 2])
        gap = sb("gap", [P, TT])
        egap = sb("egap", [P, TT])
        gden = sb("gden", [P, TT])
        gw = sb("gw", [P, TT, 2])
        oh = sb("oh", [P, 2, TT, E])
        wdense = sb("wdense", [P, TT, E])
        wt_sb = sb("wt_sb", [E, TOK])
        wbc = sb("wbc", [P, 2, E // 2, TOK])
        hid = sb("hid", [P, 8, TOK])
        prod = sb("prod", [P, 2, TOK])
        acc = sb("acc", [P, TOK])
        o_sb = sb("o_sb", [P, TT, D])

        bank = [ctx.enter_context(nc.psum_tensor(f"bank{i}", [P, 512], F32)) for i in range(8)]
        SCORE, KEYB, UPB, DOWNB = (0, 1), 3, (4, 5), 6

        def tokb(p):
            return ((2, 3), (4, 5), (2, 7), (2, 2))[p]

        def values_bank(p):
            return 7 if p == 0 else tokb(p)[1]

        def joint(p):
            return p == PAIRS - 1

        def tok_psum(p, b, t):
            if joint(p):
                return bank[tokb(p)[0]][:].rearrange("p (b l) -> p b l", b=2)
            return bank[SCORE[b] if p == 0 and t % 2 else tokb(p)[b]][:, 0:L]

        def stack_psum(p, b):
            return bank[SCORE[0] if p == 0 and b == 1 else tokb(p)[0]][0:KX, L * b:L * (b + 1)]

        def tok_batches(p, b):
            return slice(0, 2) if joint(p) else b

        def up_psum(k, i):
            banks = UPB + SCORE if k == len(UNITS) - 1 else UPB
            return bank[banks[i % len(banks)]][:, 0:UNITS[k].tok]

        def tiles(ap, u):
            if len(u.halves) == 2:
                return ap
            if len(ap.shape) == 2:
                return ap.rearrange("p (b h) -> p b h", h=2)[:, :, u.halves[0]]
            return ap.rearrange("p (b h) n -> p b h n", h=2)[:, :, u.halves[0], :]

        def tokens(ap, u):
            v = ap.rearrange("p (b t) -> p b t", b=2)
            return v[:, :, u.queries]

        def folded(k, i):
            if k == len(UNITS) - 1:
                return bank[(3, 2)[i]][:, 0:P]
            return bank[UNITS[k].fold_bank][:, P * i:P * (i + 1)]

        def product(k, ep):
            c = L * (ep // 2) if k == len(UNITS) - 1 else 0
            return prod[:, ep % 2, c:c + UNITS[k].tok]

        def packed(ap):
            return ap.rearrange("p (b t) -> p b t", b=2)

        ld_x = sem("ld_x"); ld_sel = sem("ld_sel"); ld_tok = sem("ld_tok")
        ld_wa = sem("ld_wa"); ld_att = sem("ld_att")
        ld_ffn = sem("ld_ffn")
        consts_set = sem("consts_set"); zeros_set = sem("zeros_set")
        sel_ready = sem("sel_ready"); ws_mm = sem("ws_mm")
        ws_ready = sem("ws_ready")
        xpc0_ready = sem("xpc0_ready"); xpc_ready = sem("xpc_ready"); rstd0_ready = sem("rstd0_ready")
        rstd_last_ready = sem("rstd_last_ready")
        wa_ready = sem("wa_ready"); wf_ready = sem("wf_ready"); identb_ready = sem("identb_ready")
        nbm_ready = sem("nbm_ready")
        xs_mm = sem("xs_mm"); xs_ready = sem("xs_ready")
        tok_mm = [[sem(f"tok_mm{i}{b}") for b in range(2)] for i in range(2)]
        tok_relu = [[sem(f"tok_relu{i}{b}") for b in range(2)] for i in range(2)]
        h1_mm = sem("h1_mm"); h1_ready = sem("h1_ready"); h1_stats = sem("h1_stats")
        xn1_ready = sem("xn1_ready"); xa_mm = sem("xa_mm"); xa_ready = sem("xa_ready")
        qk_mm = sem("qk_mm"); keys_mm = sem("keys_mm"); v_mm = sem("v_mm")
        qk_ready = sem("qk_ready"); v_ready = sem("v_ready")
        relu_dve = sem("relu_dve"); relu_act = sem("relu_act"); score_mm = sem("score_mm")
        score_kept = sem("score_kept"); nmx_ready = sem("nmx_ready"); exp_ready = sem("exp_ready")
        pt_mm = sem("pt_mm"); pt_ready = sem("pt_ready"); pv_mm = sem("pv_mm")
        att_ready = sem("att_ready"); att_t = sem("att_t"); h2_ready = sem("h2_ready")
        h2_stats = sem("h2_stats"); xn2_ready = sem("xn2_ready"); xf_mm = sem("xf_mm")
        xf_ready = sem("xf_ready"); gate_mm = sem("gate_mm"); lg_ready = sem("lg_ready")
        gap_ready = sem("gap_ready"); egap_ready = sem("egap_ready"); w_ready = sem("w_ready")
        wt_mm = sem("wt_mm"); wt_ready = sem("wt_ready"); wbc_ready = sem("wbc_ready")
        wbc_copied = sem("wbc_copied")
        up_mm = sem("up_mm"); gelu_ready = sem("gelu_ready"); down_mm = sem("down_mm")
        prod_ready = sem("prod_ready"); acc_ready = sem("acc_ready"); fold_mm = sem("fold_mm")
        gates_out = sem("gates_out"); out_ready = sem("out_ready"); out_stored = sem("out_stored")
        dve_step = sem("dve_step"); pool_step = sem("pool_step")

        block = ctx.enter_context(nc.Block())

        def chain(eng, step):
            count = [0]

            def link(ins):
                count[0] += 1
                ins.then_inc(step, 1)
                eng.wait_ge(step, count[0])
            return link

        def norm_split(vec, link, src, k, u=UNITS[0]):
            x, res, n = tiles(xn[:, k], u), tiles(xn_res[:, k], u), len(u.tiles)
            hi, mid, hi2, lo = (tiles(xn_pc[:, k, :, c], u) for c in range(4))
            mean, inv = tiles(mv[:, k], u)[:, :, 0:1], tiles(rstd[:, k], u)
            link(vec.tensor_tensor(x, src, mean.broadcast_to([P, n, D]), ALU.subtract))
            link(vec.tensor_tensor(x, x, inv[:, :, None].broadcast_to([P, n, D]), ALU.mult))
            link(vec.tensor_copy(hi, x))
            vec.tensor_copy(hi2, hi)
            link(vec.tensor_tensor(res, x, hi, ALU.subtract))
            link(vec.tensor_copy(mid, res))
            return vec.tensor_tensor(lo, res, mid, ALU.subtract)

        @block.sync
        def _(sp):
            def store(k):
                sp.wait_ge(out_ready, k + 1)
                u = UNITS[k]
                sp.dma_start(tiles(out_d[u.pair], u), tiles(o_sb[:], u)).then_inc(out_stored, 16)

            sp.dma_start(x_sb[:, 0], xw[:, 0]).then_inc(ld_x, 16)
            sp.dma_start(sel_f[:], sel_d).then_inc(ld_sel, 16)
            for dst, src in ((tokw_sb[:], tokw), (x_sb[:, 1:], xw[:, 1:])):
                sp.dma_start(dst, src).then_inc(ld_tok, 16)
            for dst, src in ((wa_sb[:], wa_d), (ident[:], ident_d)):
                sp.dma_start(dst, src).then_inc(ld_wa, 16)
            for dst, src in ((wsc[:], wsc_d), (bm[:], bm_d.partition_broadcast(P))):
                sp.dma_start(dst, src).then_inc(ld_att, 16)
            for dst, src in ((wf_sb[:], wf_d), (wd[:], wd_d), (b1[:], b1_d), (b2[:], b2_d),
                             (bg[:], bg_d.partition_broadcast(P)), (fold[:], fold_d),
                             (iota8[:], iota_d)):
                sp.dma_start(dst, src).then_inc(ld_ffn, 16)
            for k, u in enumerate(UNITS[:-1]):
                sp.wait_ge(wt_ready, k + 1)
                sp.dma_start(gates_dram[k, :, 0:u.tok], wt_sb[:, 0:u.tok]).then_inc(gates_out, 16)
                sp.wait_ge(gates_out, 16 * (k + 1))
                if u.pair >= 2:
                    sp.wait_ge(prod_ready, 4 * (u.pair - 1))
                for half in range(2):
                    sp.dma_start(wbc[64 * half:64 * half + 64, u.pair % 2, :, u.gate_cols],
                                 gates_dram[k, half::2, 0:u.tok].partition_broadcast(64)).then_inc(wbc_ready, 16)
                if k >= 1:
                    store(k - 1)
            store(len(UNITS) - 2)
            store(len(UNITS) - 1)
            sp.wait_ge(out_stored, 16 * len(UNITS))

        @block.gpsimd
        def _(pool):
            link = chain(pool, pool_step)
            vec = nc.gpsimd
            vec.memset(neg_half[:], -0.5)
            vec.memset(euler[:], EULER)
            vec.memset(ones32[:], 1.0)
            vec.memset(state[:, :, :, 0:1], 0.0)
            vec.memset(last[:], 0.0).then_inc(consts_set, 1)
            pool.wait_ge(consts_set, 1)

            def inv_std(k, u=UNITS[0]):
                inv = tiles(rstd[:, k], u)
                link(vec.tensor_scalar(inv, tiles(mv[:, k], u)[:, :, 1], EPS, None, ALU.add))
                return vec.tensor_tensor(inv, inv, neg_half[:, 0:len(u.tiles)], ALU.pow)

            def norm1(p):
                pool.wait_ge(h1_stats, p + 1)
                if p == 0:
                    inv_std(0).then_inc(rstd0_ready, 1)
                    return
                link(inv_std(0))
                pool.wait_ge(xa_mm, p)
                norm_split(vec, link, h1[:, p % 3], 0).then_inc(xn1_ready, 1)

            def norm2(k):
                u = UNITS[k]
                pool.wait_ge(h2_stats, k + 1)
                if u.pair >= 1:
                    pool.wait_ge(xf_mm, u.pair)
                if k == len(UNITS) - 1:
                    inv_std(1, u).then_inc(rstd_last_ready, 1)
                else:
                    link(inv_std(1, u))
                    norm_split(vec, link, tiles(h2[:, u.pair % 2], u), 1, u).then_inc(xn2_ready, 1)

            def gate_exp(k):
                u = UNITS[k]
                pool.wait_ge(gap_ready, k + 1)
                vec.tensor_tensor(tiles(egap[:], u), euler[:, 0:len(u.tiles)], tiles(gap[:], u),
                                  ALU.pow).then_inc(egap_ready, 1)

            def expert_sum(k, ep):
                n, t = 4 * k + ep, UNITS[k].tok
                pool.wait_ge(prod_ready, n + 1)
                if ep == 0:
                    if k >= 1:
                        pool.wait_ge(fold_mm, k)
                    vec.tensor_copy(acc[:, 0:t], product(k, ep)).then_inc(acc_ready, 1)
                else:
                    pool.wait_ge(acc_ready, n)
                    vec.tensor_tensor(acc[:, 0:t], acc[:, 0:t], product(k, ep),
                                      ALU.add).then_inc(acc_ready, 1)

            def input_pieces():
                x, hi, mid, lo = x_sb[:, 1:], x_pc[:, 0, 1:], x_pc[:, 1, 1:], x_pc[:, 2, 1:]
                link(vec.tensor_copy(hi, x))
                link(vec.tensor_tensor(x, x, hi, ALU.subtract))
                link(vec.tensor_copy(mid, x))
                vec.tensor_tensor(lo, x, mid, ALU.subtract).then_inc(xpc_ready, 1)

            def ffn_pieces():
                pool.wait_ge(ld_ffn, 16 * 7)
                link(vec.tensor_copy(wf_hi[:], wf_sb[:]))
                link(vec.tensor_copy(wf_lh[64:128], wf_hi[64:128]))
                link(vec.tensor_tensor(wf_sb[:], wf_sb[:], wf_hi[:], ALU.subtract))
                link(vec.tensor_copy(wf_mid[:], wf_sb[:]))
                vec.tensor_tensor(wf_lh[0:64], wf_sb[0:64], wf_mid[0:64],
                                  ALU.subtract).then_inc(wf_ready, 1)

            pool.wait_ge(ld_tok, 32)
            for n in range(FIRST, LAST):
                for p in range(PAIRS):
                    for _ in due(n, p, TOKEN_AT[p], "pool_norm"):
                        norm1(p)
                    for _ in due(n, p, TOKEN_AT[p], "pool_inputs"):
                        input_pieces()
                if n == FFN_PIECES_AT:
                    ffn_pieces()
                for k, u in enumerate(UNITS):
                    for i in due(n, u.pair, u.at, "pool_sum"):
                        expert_sum(k, i)
                    for _ in due(n, u.pair, u.at, "pool_norm"):
                        norm2(k)
                    for _ in due(n, u.pair, u.at, "pool_exp"):
                        gate_exp(k)

        @block.scalar
        def _(act):
            def stack_inputs(p):
                for b in range(2):
                    act.wait_ge(xs_mm, 2 * p + (b + 1 if p == 0 else 2))
                    nc.scalar.copy(xs[:, p % 2, L * b:L * (b + 1)], stack_psum(p, b)).then_inc(xs_ready, 1)

            def tok_step(p, t):
                act.wait_ge(tok_mm[p % 2][0], T * (p // 2) + t + 1)
                src, bs = tok_psum(p, 0, t), tok_batches(p, 0)
                if t < T - 1:
                    nc.scalar.activation(state[:, p % 2, bs, 1:L + 1], src,
                                         ACT.Relu).then_inc(tok_relu[p % 2][0], 1)
                else:
                    nc.scalar.activation(last[0:64, p % 2, bs, 1:L], src[0:64, ..., 0:L - 1],
                                         ACT.Relu).then_inc(tok_relu[p % 2][0], 1)
                    nc.scalar.activation(last[64:128, p % 2, bs, L - 2::-1], src[64:128, ..., 0:L - 1],
                                         ACT.Relu).then_inc(tok_relu[p % 2][0], 1)

            def token_out(p):
                act.wait_ge(h1_mm, p + 1)
                if p >= 3:
                    act.wait_ge(h2_ready, p - 2)
                nc.scalar.activation(h1[:, p % 3],
                                     bank[tokb(p)[0]][:].rearrange("p (t c) -> p t c", c=P)[:, :, 0:D], ACT.Relu
                                     ).then_inc(h1_ready, 1)

            def keep_qk(p):
                act.wait_ge(qk_mm, p + 1)
                if p >= 3:
                    act.wait_ge(relu_dve, SLOTS * (p - 2))
                src = bank[tokb(p)[0]]
                nc.scalar.copy(q_sb[:, p % 3, :], src[:, 0:L]).then_inc(qk_ready, 1)
                nc.scalar.mul(nk_sb[:, p % 3, :], src[:, L:2 * L], -1.0).then_inc(qk_ready, 1)

            def relu_tiles(n):
                p, g = n // SLOTS, n % SLOTS
                if n >= RING:
                    act.wait_ge(score_mm, n - RING + 1)
                keys, scale = nk_sb[:, p % 3, :], 1.0
                if g >= KEYS_FROM:
                    keys, scale = bank[KEYB][:, 0:L], -1.0
                    if g == KEYS_FROM:
                        act.wait_ge(keys_mm, p + 1)
                for m in range(8 - ACT_TILES[p][g], 8):
                    j, qi = m // 2, m % 2
                    q = (g // 8) * 64 + qi * 32 + j * 8 + g % 8
                    ins = nc.scalar.activation(relu_ring[:, n % RING, j, qi, :], keys, ACT.Relu,
                                               bias=q_sb[:, p % 3, q:q + 1], scale=scale)
                ins.then_inc(relu_act, 1)

            def exps(k, blk):
                if blk == UNITS[k].blocks[0]:
                    act.wait_ge(nmx_ready, k + 1)
                for qi in range(2):
                    c = 2 * blk + qi
                    ins = nc.scalar.activation(sc_sb[:, c, :], sc_sb[:, c, :], ACT.Exp, bias=nmx[:, c:c + 1])
                ins.then_inc(exp_ready, 1)

            def gelu(k, i):
                n, t = 16 * k + i, UNITS[k].tok
                if n == 0:
                    act.wait_ge(ld_ffn, 16 * 7)
                act.wait_ge(up_mm, n + 1)
                if n >= 8:
                    act.wait_ge(down_mm, (n - 8) // 4 + 1)
                ep, r = i // 4, i % 4
                col = (2 * ep + r % 2) * HT + r // 2
                nc.scalar.activation(hid[:, n % 8, 0:t], up_psum(k, i), ACT.Gelu,
                                     bias=b1[:, col:col + 1]).then_inc(gelu_ready, 1)

            def keep_wt(k):
                u = UNITS[k]
                t = u.tok
                act.wait_ge(wt_mm, k + 1)
                if k == len(UNITS) - 1:
                    for half, src in enumerate((u.misc, u.xf_bank)):
                        nc.scalar.copy(wbc[:, u.pair % 2, 2 * half:2 * half + 2, u.gate_cols],
                                       bank[src][:].rearrange("p (e t) -> p e t", e=2)).then_inc(wbc_copied, 1)
                    return
                if k >= 1:
                    act.wait_ge(gates_out, 16 * k)
                nc.scalar.copy(wt_sb[:, 0:t], bank[u.misc][0:E, 0:t]).then_inc(wt_ready, 1)

            act.wait_ge(ld_sel, 16)
            nc.scalar.copy(sel[:].rearrange("k s n -> k (s n)"), sel_f[:]).then_inc(sel_ready, 1)
            act.wait_ge(ws_mm, 1)
            nc.scalar.copy(ws[:], bank[tokb(0)[1]][0:KX, 0:WX]).then_inc(ws_ready, 1)
            for n in range(FIRST, LAST):
                for k, u in enumerate(UNITS):
                    for i in due(n, u.pair, u.at, "act_exp"):
                        exps(k, u.blocks[i])
                    for i in due(n, u.pair, u.at, "act_gelu"):
                        gelu(k, i)
                    for _ in due(n, u.pair, u.at, "act_wt"):
                        keep_wt(k)
                for p in range(PAIRS):
                    for _ in due(n, p, TOKEN_AT[p], "act_stack"):
                        stack_inputs(p)
                    for t in due(n, p, TOKEN_AT[p], "act_step"):
                        if not joint(p) or t % 2 == 1:
                            tok_step(p, t)
                    for _ in due(n, p, TOKEN_AT[p], "act_out"):
                        token_out(p)
                    for _ in due(n, p, TOKEN_AT[p], "act_qk"):
                        keep_qk(p)
                if 0 <= n < SLOTS * PAIRS:
                    if n % SLOTS == 0:
                        act.wait_ge(qk_ready, 2 * (n // SLOTS + 1))
                    relu_tiles(n)

        @block.vector
        def _(dve):
            link = chain(dve, dve_step)
            vec = nc.vector

            def tok_step(p, t):
                b = 0 if joint(p) else 1
                dve.wait_ge(tok_mm[p % 2][b], T * (p // 2) + t + 1)
                src, bs = tok_psum(p, b, t), tok_batches(p, b)
                if t < T - 1:
                    vec.tensor_scalar(state[:, p % 2, bs, 1:L + 1], src, 0.0, None,
                                      ALU.max).then_inc(tok_relu[p % 2][b], 1)
                else:
                    vec.tensor_scalar(last[0:64, p % 2, bs, 1:L], src[0:64, ..., 0:L - 1], 0.0, None,
                                      ALU.max).then_inc(tok_relu[p % 2][b], 1)
                    vec.tensor_scalar(last[64:128, p % 2, bs, L - 2::-1], src[64:128, ..., 0:L - 1], 0.0, None,
                                      ALU.max).then_inc(tok_relu[p % 2][b], 1)

            def token_stats(src, k, which=range(TT)):
                for i in which:
                    ins = vec.bn_stats(stats[:, k, i, :], src[:, i, :])
                link(ins)
                for i in which:
                    ins = vec.bn_aggr(mv[:, k, i, :], stats[:, k, i, :])
                return ins

            def stats1(p):
                dve.wait_ge(h1_ready, p + 1)
                if p >= 1:
                    dve.wait_ge(xn1_ready, p)
                token_stats(h1[:, p % 3], 0).then_inc(h1_stats, 1)
                if p == 0:
                    dve.wait_ge(h1_stats, 1)
                    dve.wait_ge(rstd0_ready, 1)
                    norm_split(vec, link, h1[:, 0], 0).then_inc(xn1_ready, 1)

            def keep_xa(p):
                dve.wait_ge(xa_mm, p + 1)
                if p >= 2:
                    dve.wait_ge(v_mm, p - 1)
                    dve.wait_ge(keys_mm, p - 1)
                vec.tensor_copy(xa[:, p % 2].rearrange("p a t -> p (a t)"), bank[tokb(p)[1]][:].bitcast(BF16)
                                ).then_inc(xa_ready, 1)

            def keep_v(p):
                dve.wait_ge(v_mm, p + 1)
                if p >= 3:
                    dve.wait_ge(pv_mm, p - 2)
                vec.tensor_copy(v_sb[:, p % 3].rearrange("p t g d -> p (t g d)"),
                                bank[values_bank(p)][:, 0:TT * D]).then_inc(v_ready, 1)

            def relu_tiles(n):
                p, g = n // SLOTS, n % SLOTS
                if n >= RING:
                    dve.wait_ge(score_mm, n - RING + 1)
                for m in range(8 - ACT_TILES[p][g]):
                    j, qi = m // 2, m % 2
                    q = (g // 8) * 64 + qi * 32 + j * 8 + g % 8
                    ins = vec.tensor_scalar(relu_ring[:, n % RING, j, qi, :], nk_sb[:, p % 3, :],
                                            q_sb[:, p % 3, q:q + 1], 0.0, ALU.add, ALU.max)
                ins.then_inc(relu_dve, 1)

            def keep_scores(p, blk):
                dve.wait_ge(score_mm, SLOTS * p + 8 * (blk + 1))
                if p >= 1:
                    dve.wait_ge(pt_mm, 4 * (p - 1) + blk + 1)
                    dve.wait_ge(nmx_ready, p)
                for qi in range(2):
                    c = 2 * blk + qi
                    ins = vec.tensor_scalar(sc_sb[:, c, :],
                                            bank[SCORE[blk % 2]][:, qi * L:(qi + 1) * L],
                                            neg_bm[:, 0:1], None, ALU.max, ALU.max,
                                            accum_out=mx[:, c:c + 1])
                ins.then_inc(score_kept, 1)

            def neg_max(k):
                u = UNITS[k]
                dve.wait_ge(score_kept, 4 * u.pair + u.blocks[-1] + 1)
                if u.pair >= 1:
                    dve.wait_ge(exp_ready, 4 * u.pair)
                c = slice(2 * u.blocks[0], 2 * u.blocks[-1] + 2)
                vec.tensor_scalar(nmx[:, c], mx[:, c], -1.0, None, ALU.mult).then_inc(nmx_ready, 1)

            def keep_pt(k, blk):
                u = UNITS[k]
                dve.wait_ge(pt_mm, 4 * u.pair + blk + 1)
                if u.pair >= 1 and blk == 0:
                    dve.wait_ge(pv_mm, u.pair)
                for kh in range(2):
                    ins = vec.tensor_copy(
                        pt[:, kh, :, blk].rearrange("p b q j -> p q j b"),
                        bank[u.misc][:, 256 * kh:256 * kh + 256].rearrange("p (q j b) -> p q j b", q=2, b=4))
                ins.then_inc(pt_ready, 1)

            def weigh(k):
                u = UNITS[k]
                n = P * len(u.halves)
                dve.wait_ge(pv_mm, k + 1)
                if u.pair >= 1:
                    dve.wait_ge(att_t, u.pair)
                link(vec.reciprocal(rec[:, u.queries], bank[u.misc][:, L:L + n]))
                vec.tensor_tensor(att[:, u.queries], bank[u.misc][:, 0:n], rec[:, u.queries],
                                  ALU.mult).then_inc(att_ready, 1)

            def residual1(k):
                u = UNITS[k]
                dve.wait_ge(att_t, k + 1)
                if u.pair >= 2:
                    dve.wait_ge(out_ready, u.pair - 1)
                for i, half in enumerate(u.halves):
                    src = bank[u.misc][:, P * i:P * i + P].rearrange("p (b g d) -> p b g d", b=2, g=G)
                    old = h1[:, u.pair % 3].rearrange("p (b h) (d g) -> p h b g d", h=2, g=G)[:, half]
                    new = h2[:, u.pair % 2].rearrange("p (b h) (d g) -> p h b g d", h=2, g=G)[:, half]
                    ins = vec.tensor_tensor(new, src, old, ALU.add)
                ins.then_inc(h2_ready, 1)
                dve.wait_ge(h2_ready, k + 1)
                if u.pair >= 1:
                    dve.wait_ge(xn2_ready, u.pair)
                token_stats(h2[:, u.pair % 2], 1, u.tiles).then_inc(h2_stats, 1)
                if k == len(UNITS) - 1:
                    dve.wait_ge(rstd_last_ready, 1)
                    norm_split(vec, link, tiles(h2[:, u.pair % 2], u), 1, u).then_inc(xn2_ready, 1)

            def keep_xf(k):
                u = UNITS[k]
                dve.wait_ge(xf_mm, k + 1)
                if u.pair >= 2:
                    dve.wait_ge(up_mm, 16 * (u.pair - 1))
                for s in range(2):
                    ins = vec.tensor_copy(tokens(xf[:, u.pair % 2, s, :], u),
                                          packed(bank[u.xf_bank][:].bitcast(BF16)[:, TOK * s:TOK * s + u.tok]))
                ins.then_inc(xf_ready, 1)

            def top2(k):
                u = UNITS[k]
                nt = len(u.tiles)
                if k == 0:
                    dve.wait_ge(ld_ffn, 16 * 7)
                dve.wait_ge(gate_mm, k + 1)
                vec.tensor_tensor(tiles(lg[:], u), bank[u.misc][:, 0:nt * E].rearrange("p (t e) -> p t e", e=E),
                                  bg[:, None, :].broadcast_to([P, nt, E]), ALU.add).then_inc(lg_ready, 1)
                dve.wait_ge(lg_ready, k + 1)
                for i in u.tiles:
                    ins = vec.max(top[:, i, :], lg[:, i, :])
                link(ins)
                vec.tensor_tensor(tiles(gap[:], u), tiles(top[:, :, 1], u), tiles(top[:, :, 0], u),
                                  ALU.subtract).then_inc(gap_ready, 1)
                for i in u.tiles:
                    ins = vec.max_index(topi[:, i, :], top[:, i, :], lg[:, i, :])
                link(ins)
                link(vec.tensor_copy(tiles(topf[:], u), tiles(topi[:, :, 0:2], u)))
                for c in range(2):
                    ins = vec.tensor_tensor(tiles(oh[:, c], u), iota8[:, None, :].broadcast_to([P, nt, E]),
                                            tiles(topf[:, :, c:c + 1], u).broadcast_to([P, nt, E]),
                                            ALU.is_equal)
                link(ins)

            def gate_weights(k):
                u = UNITS[k]
                nt = len(u.tiles)
                dve.wait_ge(egap_ready, k + 1)
                link(vec.tensor_scalar(tiles(gden[:], u), tiles(egap[:], u), 1.0, None, ALU.add))
                link(vec.reciprocal(tiles(gw[:, :, 0], u), tiles(gden[:], u)))
                link(vec.tensor_tensor(tiles(gw[:, :, 1], u), tiles(gw[:, :, 0], u), tiles(egap[:], u),
                                       ALU.mult))
                for c in range(2):
                    w = tiles(oh[:, c], u)
                    ins = vec.tensor_tensor(w, w, tiles(gw[:, :, c:c + 1], u).broadcast_to([P, nt, E]),
                                            ALU.mult)
                link(ins)
                vec.tensor_tensor(tiles(wdense[:], u), tiles(oh[:, 0], u), tiles(oh[:, 1], u),
                                  ALU.add).then_inc(w_ready, 1)

            def weigh_expert(k, ep):
                u = UNITS[k]
                n = 4 * k + ep
                dve.wait_ge(down_mm, n + 1)
                if k == len(UNITS) - 1:
                    dve.wait_ge(wbc_copied, ep // 2 + 1)
                    dve.wait_ge(acc_ready, 4 * k)
                else:
                    dve.wait_ge(wbc_ready, 16 * 2 * (k + 1))
                    if n >= 2:
                        dve.wait_ge(acc_ready, n - 1)
                vec.scalar_tensor_tensor(product(k, ep), bank[DOWNB][:, 0:u.tok],
                                         b2[:, ep:ep + 1], wbc[:, u.pair % 2, ep, u.gate_cols],
                                         ALU.add, ALU.mult).then_inc(prod_ready, 1)

            def residual2(k):
                u = UNITS[k]
                dve.wait_ge(fold_mm, k + 1)
                if u.pair >= 1:
                    dve.wait_ge(out_stored, 16 * u.pair)
                if k == len(UNITS) - 1:
                    for i, t in enumerate(u.tiles):
                        ins = vec.tensor_tensor(o_sb[:, t], folded(k, i)[:, 0:D], h2[:, u.pair % 2, t], ALU.add)
                    ins.then_inc(out_ready, 1)
                    return
                vec.tensor_tensor(tiles(o_sb[:], u),
                                  bank[u.fold_bank][:, 0:u.tok].rearrange("p (t c) -> p t c", c=P)[:, :, 0:D],
                                  tiles(h2[:, u.pair % 2], u), ALU.add).then_inc(out_ready, 1)

            vec.memset(zeros[:], 0.0).then_inc(zeros_set, 1)
            dve.wait_ge(ld_x, 16)
            link(vec.tensor_copy(x_pc[:, 0, 0], x_sb[:, 0]))
            link(vec.tensor_tensor(x_sb[:, 0], x_sb[:, 0], x_pc[:, 0, 0], ALU.subtract))
            link(vec.tensor_copy(x_pc[:, 1, 0], x_sb[:, 0]))
            vec.tensor_tensor(x_pc[:, 2, 0], x_sb[:, 0], x_pc[:, 1, 0],
                              ALU.subtract).then_inc(xpc0_ready, 1)
            dve.wait_ge(ld_wa, 32)
            vec.tensor_copy(ident_b[:], ident[:]).then_inc(identb_ready, 1)
            link(vec.tensor_copy(wa_hi[:], wa_sb[:]))
            vec.tensor_copy(wa_lh[64:128], wa_hi[64:128])
            link(vec.tensor_tensor(wa_sb[:], wa_sb[:], wa_hi[:], ALU.subtract))
            link(vec.tensor_copy(wa_mid[:], wa_sb[:]))
            vec.tensor_tensor(wa_lh[0:64], wa_sb[0:64], wa_mid[0:64], ALU.subtract
                              ).then_inc(wa_ready, 1)
            dve.wait_ge(ld_att, 32)
            link(vec.tensor_scalar(neg_bm[:], bm[:], -1.0, None, ALU.mult))
            dve.wait_ge(consts_set, 1)
            for n in range(FIRST, LAST):
                for p in range(PAIRS):
                    for blk in due(n, p, {"keep": KEEP_AT[p]}, "keep"):
                        keep_scores(p, blk)
                for k, u in enumerate(UNITS):
                    for _ in due(n, u.pair, u.at, "dve_neg"):
                        neg_max(k)
                    for i in due(n, u.pair, u.at, "dve_pt"):
                        keep_pt(k, u.blocks[i])
                    for _ in due(n, u.pair, u.at, "dve_weigh"):
                        weigh(k)
                    for _ in due(n, u.pair, u.at, "dve_resid"):
                        residual1(k)
                    for _ in due(n, u.pair, u.at, "dve_xf"):
                        keep_xf(k)
                    for _ in due(n, u.pair, u.at, "dve_top"):
                        top2(k)
                    for _ in due(n, u.pair, u.at, "dve_gates"):
                        gate_weights(k)
                    for i in due(n, u.pair, u.at, "dve_prod"):
                        weigh_expert(k, i)
                    for _ in due(n, u.pair, u.at, "dve_out"):
                        residual2(k)
                for p in range(PAIRS):
                    for t in due(n, p, TOKEN_AT[p], "dve_step"):
                        if not joint(p) or t % 2 == 0:
                            tok_step(p, t)
                    for _ in due(n, p, TOKEN_AT[p], "dve_stats"):
                        stats1(p)
                    for _ in due(n, p, TOKEN_AT[p], "dve_xa"):
                        keep_xa(p)
                    for _ in due(n, p, TOKEN_AT[p], "dve_v"):
                        keep_v(p)
                if 0 <= n < SLOTS * PAIRS:
                    if n % SLOTS == 0:
                        dve.wait_ge(qk_ready, 2 * (n // SLOTS + 1))
                    relu_tiles(n)

        @block.tensor
        def _(pe):
            mm = nc.tensor.matmul

            def keep_warm(n):
                for _ in range(n):
                    mm(bank[DOWNB][:], zeros[:, 0:P], zeros[:], start=True, stop=True)

            def stack_inputs(p):
                if p == 0:
                    pe.wait_ge(xpc0_ready, 1)
                else:
                    pe.wait_ge(xpc_ready, 1)
                    if p >= 2:
                        pe.wait_ge(qk_ready, 2 * FREED[p])
                        pe.wait_ge(v_ready, 1)
                for b in range(2):
                    if p >= 1 and b == 1:
                        pe.wait_ge(xs_mm, 2 * p + 1)
                    c = 1 + 2 * p + b
                    rows = slice(32 * (c % 3), 32 * (c % 3) + KR)
                    for i in range(3):
                        ins = mm(stack_psum(p, b), sel[rows, i, :], x_pc[rows, i, c // 3, :],
                                 start=(i == 0), stop=(i == 2))
                    ins.then_inc(xs_mm, 1)
                if p == 0:
                    keep_warm(WARM_STACK)

            def tok_step(p, t):
                def inputs_term(b, t):
                    rhs = xs[:, p % 2, :] if joint(p) else xs[:, p % 2, b * L:(b + 1) * L]
                    dst = bank[tokb(p)[0]][:] if joint(p) else tok_psum(p, b, t)
                    return mm(dst, ws[:, 0:P], rhs, start=(p == 0 or t == 0), stop=(p > 0 or t == 0))

                def state_term(b):
                    return mm(tok_psum(p, b, t), tokw_sb[:, 0:P], state[:, p % 2, tok_batches(p, b), 0:L],
                              start=(p > 0), stop=(p == 0))

                if t == 0 and p == 0:
                    pe.wait_ge(ws_ready, 1)
                for b in range(1 if joint(p) else 2):
                    if t == 0:
                        pe.wait_ge(xs_ready, 2 * p + (b + 1 if p == 0 else 2))
                        inputs_term(b, 0).then_inc(tok_mm[p % 2][b], 1)
                        if p == 0 and b == 1:
                            keep_warm(WARM_STEP)
                        continue
                    if p == 0 and t == 1:
                        inputs_term(b, 1)
                        if b == 0:
                            pe.wait_ge(ld_tok, 32)
                            pe.wait_ge(consts_set, 1)
                    pe.wait_ge(tok_relu[p % 2][b], (T + 1) * (p // 2) + t)
                    if p == 0:
                        state_term(b).then_inc(tok_mm[p % 2][b], 1)
                        if t < T - 1:
                            inputs_term(b, t + 1)
                    else:
                        state_term(b)
                        inputs_term(b, t).then_inc(tok_mm[p % 2][b], 1)

            def token_out(p):
                for b in range(1 if joint(p) else 2):
                    pe.wait_ge(tok_relu[p % 2][b], (T + 1) * (p // 2 + 1))
                for b in range(2):
                    for h in range(2):
                        dst = bank[tokb(p)[0]][:, P * (2 * b + h):P * (2 * b + h + 1)]
                        mm(dst, last[:, p % 2, b, P * h:P * (h + 1)], tokw_sb[:, P:2 * P], start=True, stop=False)
                        ins = mm(dst, xs[:, p % 2, b * L + P * h:b * L + P * (h + 1)], ws[:, P:2 * P],
                                 start=False, stop=True)
                ins.then_inc(h1_mm, 1)

            def transpose_pieces(dst, k, which=range(TT)):
                view = dst[:].bitcast(BF16)
                for s in range(2):
                    for i, t in enumerate(which):
                        ins = nc.tensor.transpose(view[:, TOK * s + P * i:TOK * s + P * (i + 1)],
                                                  xn_pc[:, k, t, 2 * s:2 * s + 2, :].rearrange("p a d -> p (a d)"),
                                                  ident_b[:])
                return ins

            def transpose_xn1(p):
                if p == 0:
                    pe.wait_ge(identb_ready, 1)
                pe.wait_ge(xn1_ready, p + 1)
                transpose_pieces(bank[tokb(p)[1]], 0).then_inc(xa_mm, 1)

            WA_TERMS = ((wa_hi, 0), (wa_mid, 0), (wa_lh, 1))

            def project(p):
                if p == 0:
                    pe.wait_ge(wa_ready, 1)
                    pe.wait_ge(ld_att, 32)
                pe.wait_ge(xa_ready, p + 1)
                for c in range(2):
                    for n, (w, s) in enumerate(WA_TERMS):
                        for b in range(2):
                            ins = mm(bank[tokb(p)[0]][64 * b:64 * b + 64, L * c:L * (c + 1)],
                                     w[:, D * c:D * (c + 1)], xa[:, p % 2, s, L * b:L * (b + 1)],
                                     start=(n == 0), stop=(n == 2))
                ins.then_inc(qk_mm, 1)

            def project_values(p):
                if joint(p):
                    pe.wait_ge(qk_ready, 2 * (p + 1))
                for i in range(TT):
                    for n, (w, s) in enumerate(WA_TERMS):
                        ins = mm(bank[values_bank(p)][:, D * i:D * (i + 1)], xa[:, p % 2, s, P * i:P * (i + 1)],
                                 w[:, 2 * D:3 * D], start=(n == 0), stop=(n == 2))
                ins.then_inc(v_mm, 1)

            def project_keys(p):
                if p == 0:
                    pe.wait_ge(xa_ready, 1)
                else:
                    pe.wait_ge(relu_act, SLOTS * p)
                for n, (w, s) in enumerate(WA_TERMS):
                    for b in range(2):
                        ins = mm(bank[KEYB][64 * b:64 * b + 64, 0:L], w[:, D:2 * D],
                                 xa[:, p % 2, s, L * b:L * (b + 1)], start=(n == 0), stop=(n == 2))
                ins.then_inc(keys_mm, 1)

            def scores(n):
                p, g = n // SLOTS, n % SLOTS
                blk, s = g // 8, g % 8
                if s == 0 and 4 * p + blk >= 2:
                    pe.wait_ge(score_kept, 4 * p + blk - 1)
                pe.wait_ge(relu_dve, n + 1)
                pe.wait_ge(relu_act, n + 1)
                for j in range(4):
                    ins = mm(bank[SCORE[blk % 2]][32 * j:32 * j + 32, :], wsc[:, s, :],
                             relu_ring[:, n % RING, j].rearrange("p q k -> p (q k)"),
                             start=(s == 0), stop=(s == 7))
                ins.then_inc(score_mm, 1)

            def transpose_probs(k, blk):
                u = UNITS[k]
                pe.wait_ge(exp_ready, 4 * u.pair + blk + 1)
                if blk != u.blocks[0]:
                    pe.wait_ge(pt_ready, 4 * u.pair + blk)
                elif k == 0:
                    pe.wait_ge(v_ready, 3)
                elif u.pair < PAIRS - 1:
                    pe.wait_ge(wt_ready, k)
                elif k == len(UNITS) - 2:
                    pe.wait_ge(v_ready, PAIRS)
                    pe.wait_ge(qk_ready, 2 * PAIRS)
                elif k == len(UNITS) - 1:
                    pe.wait_ge(wt_ready, k - 1)
                for kh in range(2):
                    for qi in range(2):
                        ins = nc.tensor.transpose(
                            bank[u.misc][:, P * (2 * kh + qi):P * (2 * kh + qi + 1)],
                            sc_sb[:, 2 * blk + qi, P * kh:P * (kh + 1)], ident[:])
                ins.then_inc(pt_mm, 1)

            def attend(k):
                u = UNITS[k]
                n = P * len(u.halves)
                pe.wait_ge(pt_ready, 4 * u.pair + u.blocks[-1] + 1)
                pe.wait_ge(v_ready, u.pair + 1)
                for part in range(2):
                    for kh in range(2):
                        for r in range(4):
                            lhs = v_sb[:, u.pair % 3, 2 * (r // 2) + kh, r % 2, :] if part == 0 else ones32[:]
                            ins = mm(bank[u.misc][32 * r:32 * r + 32, L * part:L * part + n], lhs,
                                     pt[:, kh, r, u.blocks[0]:u.blocks[-1] + 1].rearrange("p b q j -> p (b q j)"),
                                     start=(kh == 0), stop=(kh == 1))
                ins.then_inc(pv_mm, 1)

            def transpose_att(k):
                u = UNITS[k]
                pe.wait_ge(att_ready, k + 1)
                for i, half in enumerate(u.halves):
                    ins = nc.tensor.transpose(bank[u.misc][:, P * i:P * (i + 1)],
                                              att[:, P * half:P * (half + 1)], ident[:])
                ins.then_inc(att_t, 1)

            def transpose_xn2(k):
                u = UNITS[k]
                pe.wait_ge(xn2_ready, k + 1)
                if u.xf_bank == DOWNB:
                    if k >= 1:
                        pe.wait_ge(out_ready, k)
                elif k == len(UNITS) - 2:
                    pe.wait_ge(relu_act, SLOTS * PAIRS)
                else:
                    pe.wait_ge(xf_ready, k)
                transpose_pieces(bank[u.xf_bank], 1, u.tiles).then_inc(xf_mm, 1)

            def gate(k):
                u = UNITS[k]
                if k == 0:
                    pe.wait_ge(wf_ready, 1)
                    pe.wait_ge(ld_ffn, 16 * 7)
                    pe.wait_ge(qk_ready, 4)
                    pe.wait_ge(v_ready, 2)
                pe.wait_ge(xf_ready, k + 1)
                pe.wait_ge(h2_ready, k + 1)
                for i, t in enumerate(u.tiles):
                    for n, (w, s) in enumerate(((wf_hi, 0), (wf_mid, 0), (wf_lh, 1))):
                        ins = mm(bank[u.misc][:, E * i:E * (i + 1)], xf[:, u.pair % 2, s, P * t:P * (t + 1)],
                                 w[:, E * H:], start=(n == 0), stop=(n == 2))
                ins.then_inc(gate_mm, 1)

            def transpose_gates(k):
                u = UNITS[k]
                pe.wait_ge(w_ready, k + 1)
                if k == len(UNITS) - 1:
                    for ep in range(E // 2):
                        dst = bank[(u.misc, u.xf_bank)[ep // 2]]
                        for i, t in enumerate(u.tiles):
                            c = L * (ep % 2) + P * i
                            for e2 in range(2):
                                ins = mm(dst[64 * e2:64 * e2 + 64, c:c + P],
                                         wdense[:, t, 2 * ep + e2:2 * ep + e2 + 1].broadcast_to([P, D]),
                                         ident[:], start=True, stop=True)
                    ins.then_inc(wt_mm, 1)
                    return
                for i, t in enumerate(u.tiles):
                    ins = nc.tensor.transpose(bank[u.misc][0:E, P * i:P * (i + 1)], wdense[:, t, :], ident[:])
                ins.then_inc(wt_mm, 1)

            def up(k, i):
                u = UNITS[k]
                n = 16 * k + i
                if k < len(UNITS) - 1:
                    if n >= 2:
                        pe.wait_ge(gelu_ready, n - 1)
                elif i < 2:
                    pe.wait_ge(gelu_ready, n - 1)
                elif i < 4:
                    pe.wait_ge(score_kept, 4 * PAIRS)
                else:
                    pe.wait_ge(gelu_ready, n - 3)
                ep, r = i // 4, i % 4
                col = (2 * ep + r % 2) * H + (r // 2) * P
                for c, (w, s) in enumerate(((wf_hi, 0), (wf_mid, 0), (wf_lh, 1))):
                    ins = mm(packed(up_psum(k, i)), w[:, col:col + P], tokens(xf[:, u.pair % 2, s, :], u),
                             start=(c == 0), stop=(c == 2))
                ins.then_inc(up_mm, 1)

            def down(k, ep):
                u = UNITS[k]
                n = 4 * k + ep
                pe.wait_ge(gelu_ready, 4 * (n + 1))
                if n >= 1:
                    pe.wait_ge(prod_ready, n)
                if ep == 0 and k >= 1 and UNITS[k - 1].fold_bank == DOWNB:
                    pe.wait_ge(out_ready, k)
                for ht in range(HT):
                    for e2 in range(2):
                        ins = mm(bank[DOWNB][64 * e2:64 * e2 + 64, 0:u.tok], wd[:, 2 * ep + e2, ht, :],
                                 hid[:, (4 * n + 2 * ht + e2) % 8, 0:u.tok], start=(ht == 0), stop=(ht == HT - 1))
                ins.then_inc(down_mm, 1)

            def fold_experts(k, ep):
                u = UNITS[k]
                last_unit = k == len(UNITS) - 1
                if last_unit:
                    if ep == 0:
                        pe.wait_ge(out_ready, k)
                        pe.wait_ge(wbc_copied, 2)
                    pe.wait_ge(prod_ready, 4 * k + ep + 1)
                else:
                    pe.wait_ge(acc_ready, 4 * (k + 1))
                    if k == len(UNITS) - 3:
                        pe.wait_ge(wt_ready, k + 2)
                    elif k == len(UNITS) - 2:
                        pe.wait_ge(out_ready, k)
                for i in range(len(u.tiles)):
                    lhs = product(k, ep) if last_unit else acc
                    ins = mm(folded(k, i), lhs[:, P * i:P * (i + 1)], fold[:],
                             start=(not last_unit or ep == 0), stop=(not last_unit or ep == 3))
                if not last_unit or ep == 3:
                    ins.then_inc(fold_mm, 1)

            pe.wait_ge(sel_ready, 1)
            pe.wait_ge(xpc0_ready, 1)
            for j in range(3):
                ins = mm(bank[tokb(0)[1]][0:KX, 0:WX], sel[0:KR, 3 + j, :], x_pc[0:KR, j, 0, :],
                         start=(j == 0), stop=(j == 2))
            ins.then_inc(ws_mm, 1)
            for n in range(FIRST, LAST):
                for k, u in enumerate(UNITS):
                    for i in due(n, u.pair, u.at, "pe_probs"):
                        transpose_probs(k, u.blocks[i])
                    for _ in due(n, u.pair, u.at, "pe_attend"):
                        attend(k)
                    for _ in due(n, u.pair, u.at, "pe_att_t"):
                        transpose_att(k)
                    for _ in due(n, u.pair, u.at, "pe_xf"):
                        transpose_xn2(k)
                    for _ in due(n, u.pair, u.at, "pe_gate"):
                        gate(k)
                    for i in due(n, u.pair, u.at, "pe_up"):
                        up(k, i)
                    for i in due(n, u.pair, u.at, "pe_down"):
                        down(k, i)
                    for _ in due(n, u.pair, u.at, "pe_gates_t"):
                        transpose_gates(k)
                    for i in due(n, u.pair, u.at, "pe_fold"):
                        fold_experts(k, i)
                for p in range(PAIRS):
                    for _ in due(n, p, TOKEN_AT[p], "pe_stack"):
                        stack_inputs(p)
                    for t in due(n, p, TOKEN_AT[p], "pe_step"):
                        tok_step(p, t)
                    for _ in due(n, p, TOKEN_AT[p], "pe_out"):
                        token_out(p)
                    for _ in due(n, p, TOKEN_AT[p], "pe_xa"):
                        transpose_xn1(p)
                    for _ in due(n, p, TOKEN_AT[p], "pe_project"):
                        project(p)
                    for _ in due(n, p, TOKEN_AT[p], "pe_values"):
                        project_values(p)
                    for _ in due(n, p, TOKEN_AT[p], "pe_keys"):
                        project_keys(p)
                if 0 <= n - LAG < SLOTS * PAIRS:
                    scores(n - LAG)


def kernel(x, L0_tok_W1, L0_tok_b1, L0_tok_W2, L0_tok_b2, L0_tok_W3, L0_tok_b3, L0_tok_W4, L0_tok_b4,
           L0_attn_Wq, L0_attn_Wk, L0_attn_Wv, L0_attn_w_mlp, L0_attn_b_mlp, L0_ffn_Wg, L0_ffn_bg,
           L0_ffn_W1, L0_ffn_b1, L0_ffn_W2, L0_ffn_b2):
    import numpy as np
    import concourse.bacc as bacc
    from concourse.bass_utils import run_bass_kernel_spmd

    f = lambda a: np.asarray(a)
    x, W1, W2, W3, W4 = f(x), f(L0_tok_W1), f(L0_tok_W2), f(L0_tok_W3), f(L0_tok_W4)
    arrays = {}
    w = np.zeros((KR, WX), np.float32)
    w[0:4, 0:64] = W1.T
    w[4:8, 64:128] = W1.T
    for at in (0, 64):
        w[0:4, 128 + at:192 + at] = W3.T
        w[8, at:at + 64] = f(L0_tok_b1)
        w[9, at:at + 64] = f(L0_tok_b2)
        w[8, 128 + at:192 + at] = f(L0_tok_b3)
        w[9:11, 128 + at:192 + at] = f(L0_tok_b4)
    xw = np.zeros((GROUPS, 32, 3, L), np.float32)
    xw[0, 0:KR, 0] = w
    for b in range(B):
        c = 1 + b
        xw[c % 3, 0:4, c // 3] = x[b]
        xw[c % 3, 4:8, c // 3] = x[b, :, ::-1]
        xw[c % 3, 8:KR, c // 3] = 1
    arrays["xw"] = xw.reshape(32 * GROUPS, 3, L)
    sel = np.zeros((GROUPS, 32, 6, KX), np.float32)
    for j in range(3):
        for i in range(3):
            for r in range(8):
                sel[:, r, i, 24 * i + 8 * j + r] = 1
                sel[:, r, 3 + j, 24 * i + 8 * j + r] = 1
        for r in range(3):
            sel[:, 8 + r, 0, 72 + 3 * j + r] = 1
            sel[:, 8 + r, 3 + j, 72 + 3 * j + r] = 1
    arrays["sel"] = sel.reshape(32 * GROUPS, -1)
    tokw = np.zeros((P, 2 * P), np.float32)
    tokw[0:64, 0:64] = W2.T
    tokw[64:128, 64:128] = W2.T
    for r in (0, 64):
        for c in (128, 192):
            tokw[r:r + 64, c:c + 64] = W4.T
    arrays["tokw"] = tokw
    arrays["ident"] = np.eye(P, dtype=np.float32)
    arrays["fold"] = np.tile(np.eye(D, dtype=np.float32), (2, 2))
    arrays["iota"] = np.tile(np.arange(E, dtype=np.float32), (P, 1))
    wv = f(L0_attn_Wv).reshape(DG, G, D).transpose(1, 0, 2).reshape(D, D)
    wa = np.concatenate([f(L0_attn_Wq).T, f(L0_attn_Wk).T, wv.T], 1)
    arrays["wa"] = np.concatenate([wa, wa])
    wf = np.concatenate([f(L0_ffn_W1).transpose(1, 0, 2).reshape(D, E * H), f(L0_ffn_Wg)], 1)
    arrays["wf"] = np.concatenate([wf, wf])
    arrays["wd"] = f(L0_ffn_W2).reshape(E, HT, P, D).transpose(2, 0, 1, 3)
    arrays["b1"] = f(L0_ffn_b1).reshape(E, HT, P).transpose(2, 0, 1).reshape(P, E * HT)
    arrays["b2"] = f(L0_ffn_b2).reshape(E // 2, 2, D).transpose(1, 2, 0).reshape(P, E // 2)
    arrays["bg"] = f(L0_ffn_bg)
    arrays["bm"] = f(L0_attn_b_mlp)
    wsc = np.zeros((P, 8, 32), np.float32)
    for r in range(4):
        for s in range(8):
            wsc[32 * r:32 * r + 32, s, 4 * s + r] = f(L0_attn_w_mlp)
    arrays["wsc"] = wsc

    nc = bacc.Bacc("TRN2", target_bir_lowering=False, num_devices=1)
    arrays = {f"in_{k}": np.ascontiguousarray(a) for k, a in arrays.items()}
    args = [nc.dram_tensor(k, a.shape, mybir.dt.from_np(a.dtype), kind="ExternalInput").ap()
            for k, a in arrays.items()]
    out = nc.dram_tensor("out", (PAIRS, P, TT, D), F32, kind="ExternalOutput").ap()
    gates = nc.dram_tensor("gates", (len(UNITS), E, TOK), F32, kind="Internal").ap()
    build(nc, *args, gates, out)
    r = run_bass_kernel_spmd(nc, [arrays], core_ids=[0])
    got = r.results[0]["out"]
    return np.ascontiguousarray(got.transpose(0, 2, 1, 3)).reshape(B, L, D)
```
